# Optimizing a Trainium2 kernel written in Bass

```python
import numpy as np
import jax
import jax.numpy as jnp

def _softmax(x, axis=-1):
    return jax.nn.softmax(x, axis=axis)

def _gelu(x):
    return jax.nn.gelu(x, approximate=True)

def _silu(x):
    return jax.nn.silu(x)

def _sigmoid(x):
    return jax.nn.sigmoid(x)

def _layernorm(x, axis=-1, eps=1e-05):
    m = jnp.mean(x, axis=axis, keepdims=True)
    v = jnp.var(x, axis=axis, keepdims=True)
    return (x - m) / jnp.sqrt(v + eps)

def _scatter_add(tgt, idx, src, axis=0):
    return tgt.at[idx].add(src)

def _segment_sum(src, seg, n):
    return jax.ops.segment_sum(src, seg, n)
kernel_name = 'mk_flamingo_gated_d1_seqx_r4_88210a'

def setup_inputs(seed: int=0):
    np.random.seed(seed)
    _w = jnp.asarray

    def _rec_inputs():
        import jax
        import jax.numpy as jnp
        _rk = jax.random.key(seed)
        x = 4.136e-05 + 0.9999 * jax.random.normal(jax.random.fold_in(_rk, 1), (4, 512, 512), jnp.float32)
        _lenS = 512 - jax.random.randint(jax.random.fold_in(_rk, 7), (4,), 0, max(1, 512 // 4) + 1, jnp.int32)
        _lenS2 = 512 - jax.random.randint(jax.random.fold_in(_rk, 8), (4,), 0, max(1, 512 // 4) + 1, jnp.int32)
        _ctx_1024P = jax.random.normal(jax.random.fold_in(_rk, 11), (4, 16, 256), jnp.float32)
        _ctx_1024c = jax.random.dirichlet(jax.random.fold_in(_rk, 511), 0.3 * jnp.ones((16,), jnp.float32), (4, 512))
        _ctx_1024t = jnp.einsum('bsk,bkd->bsd', _ctx_1024c, _ctx_1024P)
        _ctx_1024t = _ctx_1024t * jax.lax.rsqrt(jnp.mean(jnp.square(_ctx_1024t)) + 1e-12) * 0.953939
        ctx_1024 = -0.000292821 + 1.00034 * (_ctx_1024t + 0.3 * jax.random.normal(jax.random.fold_in(_rk, 611), (4, 512, 256), jnp.float32))
        _g = jax.random.normal(jax.random.fold_in(_rk, 9001), (2, 1), jnp.float32)
        _g = jnp.sign(_g) * jnp.maximum(jnp.abs(_g), 1.0) + (_g == 0) * 1.0
        g_xattn = _g[0]
        g_ffn = _g[1]
        return (x, ctx_1024, g_xattn, g_ffn)
    x, ctx_1024, g_xattn, g_ffn = _rec_inputs()

    def _L0_xattn_setup():
        import jax, jax.numpy as jnp
        import numpy as np
        import math
        B, L, DM = (2, 512, 256)
        DS, DC, EXP = (16, 4, 2)
        DI = EXP * DM
        DR = math.ceil(DM / 16)
        DT_MIN, DT_MAX, DT_FLOOR = (0.001, 0.1, 0.0001)

        def _ssm_forward(hidden_states, z, in_proj_w, conv_w, conv_b, x_proj_w, dt_proj_w, dt_proj_b, A_log, D):
            b = hidden_states.shape[0]
            x = jnp.einsum('ed,bld->bel', in_proj_w, hidden_states)
            xp = jnp.pad(x, ((0, 0), (0, 0), (DC - 1, 0)))
            xc = jax.lax.conv_general_dilated(xp, conv_w[:, None, :], window_strides=(1,), padding='VALID', dimension_numbers=('NCH', 'OIH', 'NCH'), feature_group_count=DI)
            u = jax.nn.silu(xc + conv_b[None, :, None])
            x_dbl = jnp.einsum('ke,bel->bkl', x_proj_w, u)
            dt_lo = x_dbl[:, :DR]
            Bm = x_dbl[:, DR:DR + DS]
            Cm = x_dbl[:, DR + DS:]
            delta = jax.nn.softplus(jnp.einsum('er,brl->bel', dt_proj_w, dt_lo) + dt_proj_b[None, :, None])
            A = -jnp.exp(A_log)

            def step(state, xs):
                d_t, B_t, C_t, u_t = xs
                dA = jnp.exp(d_t[..., None] * A)
                state = state * dA + (d_t * u_t)[..., None] * B_t[:, None, :]
                y_t = jnp.einsum('ben,bn->be', state, C_t)
                return (state, y_t)
            xs = (jnp.moveaxis(delta, -1, 0), jnp.moveaxis(Bm, -1, 0), jnp.moveaxis(Cm, -1, 0), jnp.moveaxis(u, -1, 0))
            state0 = jnp.zeros((b, DI, DS), delta.dtype)
            _, ys = jax.lax.scan(step, state0, xs)
            y = jnp.moveaxis(ys, 0, -1)
            y = y + D[None, :, None] * u
            y = y * jax.nn.silu(z)
            return jnp.swapaxes(y, 1, 2)
        key = jax.random.key(seed)
        ks = jax.random.split(key, 8)
        hidden_states = jax.random.normal(ks[0], (B, L, DM), jnp.float32)
        z = jax.random.normal(ks[1], (B, DI, L), jnp.float32)
        in_proj_w = jax.random.normal(ks[2], (DI, DM), jnp.float32) * DM ** (-0.5)
        conv_w = jax.random.normal(ks[3], (DI, DC), jnp.float32) * DC ** (-0.5)
        conv_b = jnp.zeros((DI,), jnp.float32)
        x_proj_w = jax.random.normal(ks[4], (DR + 2 * DS, DI), jnp.float32) * DI ** (-0.5)
        dt_std = DR ** (-0.5)
        dt_proj_w = jax.random.uniform(ks[5], (DI, DR), jnp.float32, -dt_std, dt_std)
        dt = jnp.exp(jax.random.uniform(ks[6], (DI,), jnp.float32) * (math.log(DT_MAX) - math.log(DT_MIN)) + math.log(DT_MIN))
        dt = jnp.clip(dt, DT_FLOOR)
        dt_proj_b = dt + jnp.log(-jnp.expm1(-dt))
        A_log = jnp.log(jnp.broadcast_to(jnp.arange(1, DS + 1, dtype=jnp.float32), (DI, DS)))
        D = jnp.ones((DI,), jnp.float32)
        return dict(hidden_states=hidden_states, z=z, in_proj_w=in_proj_w, conv_w=conv_w, conv_b=conv_b, x_proj_w=x_proj_w, dt_proj_w=dt_proj_w, dt_proj_b=dt_proj_b, A_log=A_log, D=D)
    _L0_xattn_all = _L0_xattn_setup()
    _L0_xattn_in = {k: v for k, v in _L0_xattn_all.items() if k in ('in_proj_w', 'conv_w', 'conv_b', 'x_proj_w', 'dt_proj_w', 'dt_proj_b', 'A_log', 'D')}
    del _L0_xattn_all

    def _L0_ffn_setup():
        import jax, jax.numpy as jnp
        import numpy as np
        NUM_EXPERTS = 8
        TOP_K = 2
        IN_DIM = 512
        BOT_DIM = 128
        BATCH, SEQ = (4, 512)

        def _gelu(x):
            return jax.nn.gelu(x, approximate=False)
        key = jax.random.key(seed)
        ks = jax.random.split(key, 8)
        scale_d = 1.0 / np.sqrt(IN_DIM)
        scale_b = 1.0 / np.sqrt(BOT_DIM)
        return {'hidden_states': jax.random.normal(ks[0], (BATCH, SEQ, IN_DIM), jnp.float32), 'gate_w': jax.random.normal(ks[1], (NUM_EXPERTS, IN_DIM), jnp.float32) * scale_d, 'wd': jax.random.normal(ks[2], (NUM_EXPERTS, BOT_DIM, IN_DIM), jnp.float32) * scale_d, 'bd': jnp.zeros((NUM_EXPERTS, BOT_DIM), jnp.float32), 'wu': jax.random.normal(ks[3], (NUM_EXPERTS, IN_DIM, BOT_DIM), jnp.float32) * scale_b * 0.02, 'bu': jnp.zeros((NUM_EXPERTS, IN_DIM), jnp.float32), 'ws_d': jax.random.normal(ks[4], (BOT_DIM, IN_DIM), jnp.float32) * scale_d, 'bs_d': jnp.zeros((BOT_DIM,), jnp.float32), 'ws_u': jax.random.normal(ks[5], (IN_DIM, BOT_DIM), jnp.float32) * scale_b * 0.02, 'bs_u': jnp.zeros((IN_DIM,), jnp.float32)}
    _L0_ffn_all = _L0_ffn_setup()
    _L0_ffn_in = {k: v for k, v in _L0_ffn_all.items() if k in ('gate_w', 'wd', 'bd', 'wu', 'bu', 'ws_d', 'bs_d', 'ws_u', 'bs_u')}
    del _L0_ffn_all
    return {'x': x, 'ctx_1024': ctx_1024, 'g_xattn': g_xattn, 'g_ffn': g_ffn, 'L0_xattn_in_proj_w': _L0_xattn_in['in_proj_w'], 'L0_xattn_conv_w': _L0_xattn_in['conv_w'], 'L0_xattn_conv_b': _L0_xattn_in['conv_b'], 'L0_xattn_x_proj_w': _L0_xattn_in['x_proj_w'], 'L0_xattn_dt_proj_w': _L0_xattn_in['dt_proj_w'], 'L0_xattn_dt_proj_b': _L0_xattn_in['dt_proj_b'], 'L0_xattn_A_log': _L0_xattn_in['A_log'], 'L0_xattn_D': _L0_xattn_in['D'], 'L0_ffn_gate_w': _L0_ffn_in['gate_w'], 'L0_ffn_wd': _L0_ffn_in['wd'], 'L0_ffn_bd': _L0_ffn_in['bd'], 'L0_ffn_wu': _L0_ffn_in['wu'], 'L0_ffn_bu': _L0_ffn_in['bu'], 'L0_ffn_ws_d': _L0_ffn_in['ws_d'], 'L0_ffn_bs_d': _L0_ffn_in['bs_d'], 'L0_ffn_ws_u': _L0_ffn_in['ws_u'], 'L0_ffn_bs_u': _L0_ffn_in['bs_u']}

def reference(x, ctx_1024, g_xattn, g_ffn, L0_xattn_in_proj_w, L0_xattn_conv_w, L0_xattn_conv_b, L0_xattn_x_proj_w, L0_xattn_dt_proj_w, L0_xattn_dt_proj_b, L0_xattn_A_log, L0_xattn_D, L0_ffn_gate_w, L0_ffn_wd, L0_ffn_bd, L0_ffn_wu, L0_ffn_bu, L0_ffn_ws_d, L0_ffn_bs_d, L0_ffn_ws_u, L0_ffn_bs_u):
    import jax
    import jax.numpy as jnp

    def _L0_xattn_ref(hidden_states, z, in_proj_w, conv_w, conv_b, x_proj_w, dt_proj_w, dt_proj_b, A_log, D):
        import jax, jax.numpy as jnp
        import numpy as np
        import math
        B, L, DM = (2, 512, 256)
        DS, DC, EXP = (16, 4, 2)
        DI = EXP * DM
        DR = math.ceil(DM / 16)
        DT_MIN, DT_MAX, DT_FLOOR = (0.001, 0.1, 0.0001)

        def _ssm_forward(hidden_states, z, in_proj_w, conv_w, conv_b, x_proj_w, dt_proj_w, dt_proj_b, A_log, D):
            b = hidden_states.shape[0]
            x = jnp.einsum('ed,bld->bel', in_proj_w, hidden_states)
            xp = jnp.pad(x, ((0, 0), (0, 0), (DC - 1, 0)))
            xc = jax.lax.conv_general_dilated(xp, conv_w[:, None, :], window_strides=(1,), padding='VALID', dimension_numbers=('NCH', 'OIH', 'NCH'), feature_group_count=DI)
            u = jax.nn.silu(xc + conv_b[None, :, None])
            x_dbl = jnp.einsum('ke,bel->bkl', x_proj_w, u)
            dt_lo = x_dbl[:, :DR]
            Bm = x_dbl[:, DR:DR + DS]
            Cm = x_dbl[:, DR + DS:]
            delta = jax.nn.softplus(jnp.einsum('er,brl->bel', dt_proj_w, dt_lo) + dt_proj_b[None, :, None])
            A = -jnp.exp(A_log)

            def step(state, xs):
                d_t, B_t, C_t, u_t = xs
                dA = jnp.exp(d_t[..., None] * A)
                state = state * dA + (d_t * u_t)[..., None] * B_t[:, None, :]
                y_t = jnp.einsum('ben,bn->be', state, C_t)
                return (state, y_t)
            xs = (jnp.moveaxis(delta, -1, 0), jnp.moveaxis(Bm, -1, 0), jnp.moveaxis(Cm, -1, 0), jnp.moveaxis(u, -1, 0))
            state0 = jnp.zeros((b, DI, DS), delta.dtype)
            _, ys = jax.lax.scan(step, state0, xs)
            y = jnp.moveaxis(ys, 0, -1)
            y = y + D[None, :, None] * u
            y = y * jax.nn.silu(z)
            return jnp.swapaxes(y, 1, 2)
        return _ssm_forward(hidden_states, z, in_proj_w, conv_w, conv_b, x_proj_w, dt_proj_w, dt_proj_b, A_log, D)

    def _L0_ffn_ref(hidden_states, gate_w, wd, bd, wu, bu, ws_d, bs_d, ws_u, bs_u):
        import jax, jax.numpy as jnp
        import numpy as np
        NUM_EXPERTS = 8
        TOP_K = 2
        IN_DIM = 512
        BOT_DIM = 128
        BATCH, SEQ = (4, 512)

        def _gelu(x):
            return jax.nn.gelu(x, approximate=False)
        B, S, D = hidden_states.shape
        x = hidden_states.reshape(-1, D)
        T = x.shape[0]
        logits = x @ gate_w.T
        probs = jax.nn.softmax(logits.astype(jnp.float32), axis=-1)
        rw, sel = jax.lax.top_k(probs, TOP_K)
        rw = rw / rw.sum(axis=-1, keepdims=True)
        rw = rw.astype(x.dtype)
        combine = jnp.zeros((T, NUM_EXPERTS), x.dtype).at[jnp.arange(T)[:, None], sel].add(rw)
        down = jnp.einsum('td,ebd->teb', x, wd) + bd[None]
        h = _gelu(down) * combine[:, :, None]
        expert_out = jnp.einsum('teb,edb->td', h, wu) + combine @ bu
        shared = _gelu(x @ ws_d.T + bs_d) @ ws_u.T + bs_u
        out = (expert_out + shared).reshape(B, S, D)
        return out
    x = x + jnp.tanh(g_xattn[0]) * _L0_xattn_ref(ctx_1024, _layernorm(x, axis=-1), L0_xattn_in_proj_w, L0_xattn_conv_w, L0_xattn_conv_b, L0_xattn_x_proj_w, L0_xattn_dt_proj_w, L0_xattn_dt_proj_b, L0_xattn_A_log, L0_xattn_D)
    x = x + jnp.tanh(g_ffn[0]) * _L0_ffn_ref(_layernorm(x, axis=-1), L0_ffn_gate_w, L0_ffn_wd, L0_ffn_bd, L0_ffn_wu, L0_ffn_bu, L0_ffn_ws_d, L0_ffn_bs_d, L0_ffn_ws_u, L0_ffn_bs_u)
    return x

_drawn_inputs = setup_inputs


def setup_inputs(seed=0):
    import zlib

    import numpy as np

    out = dict(_drawn_inputs(seed))
    spreads = {'L0_xattn_conv_b': (0.0, 0.269),
     'L0_xattn_D': (1.0, 0.2),
     'L0_ffn_bd': (0.0, 0.8),
     'L0_ffn_bu': (0.0, 0.1),
     'L0_ffn_bs_d': (0.0, 0.8),
     'L0_ffn_bs_u': (0.0, 0.1)}
    factors = {'L0_xattn_dt_proj_w': 6.298,
     'L0_xattn_dt_proj_b': 2.841,
     'L0_ffn_wd': 7.133,
     'L0_ffn_wu': 6.428,
     'L0_ffn_ws_d': 5.293,
     'L0_ffn_ws_u': 4.783}
    for name, (base, spread) in spreads.items():
        noise = np.random.default_rng([zlib.crc32(name.encode()), seed]).standard_normal(out[name].shape)
        drawn = base * np.exp(spread * noise) if base else spread * noise
        out[name] = jnp.asarray(drawn.astype(out[name].dtype))
    for name, factor in factors.items():
        out[name] = (out[name] * factor).astype(out[name].dtype)
    return out
```

```python
from contextlib import ExitStack

import concourse.bass as bass
from concourse import mybir

ALU = mybir.AluOpType
ACT = mybir.ActivationFunctionType
F32 = mybir.dt.float32
U32 = mybir.dt.uint32

P = 128
NB = 4
L = 512
DM = 512
DCTX = 256
KC = DCTX // P
NW = DM // P
NS = 16
PAIR = 2
NG = NS // PAIR
GB = NW * NG
R = 16
TAPS = 4
NX = 8
NE = NX + 1
NT = L // P
RING = 4
LAG = 2
LOW = 64
EPS = 1e-5
DMA = 16
INPROJ_SLOT = (2, 0, 0, 0)
CONV_SLOT = (3, 2, 2, 2)
POOL_CONSTS = 7 + NX
ROUTE_STEPS = 13
GELU_EVERY = 3


def jobs_of_slot(b, c, g):
    prep, ffn, scan = b_prep(b), b_ffn(b), b_scan(b)
    jobs = []
    if prep and g == INPROJ_SLOT[c]:
        jobs.append(("in_proj", c))
    if prep and g == CONV_SLOT[c]:
        jobs.append(("conv", c))
    if prep and c == NW - 1 and g == 3:
        jobs.append(("x_proj", 0))
    if g == 5 and (scan or c == NW - 1) and not is_int(b, NB) and not (is_int(b, NB - 1) and c == NW - 1):
        jobs.append(("dt", c))
    if ffn:
        if c == 0:
            jobs += {4: [("mean", 0)], 5: [("var", 0)], 7: [("logits", 0)]}.get(g, [])
        if c == 1:
            jobs += ([("comb", 0)] if g == 0 else []) + [("down", g)]
        if c == 2:
            jobs += {0: [("down", 8)], 5: [("up", 0)], 7: [("up", 1)]}.get(g, [])
            if 1 <= g <= 4:
                jobs += [("mix", 2 * g - 2), ("mix", 2 * g - 1)]
        if c == 3:
            jobs += {1: [("up", 2)], 5: [("up", 3)]}.get(g, [])
    return jobs


def is_int(b, value):
    return isinstance(b, int) and b == value


def b_prep(b):
    return not (isinstance(b, int) and b >= NB - 1)


def b_ffn(b):
    return not (isinstance(b, int) and b <= 0)


def b_scan(b):
    return not (isinstance(b, int) and (b < 0 or b == NB))


def jobs_of_body(b):
    return [j for c in range(NW) for g in range(NG) for j in jobs_of_slot(b, c, g)]


BEFORE_FIRST = len(jobs_of_body(-1))
BEFORE_FULL = BEFORE_FIRST + len(jobs_of_body(0))
PER_FULL = len(jobs_of_body(1))
assert PER_FULL % 2 == 0
ORDER = {b: jobs_of_body(b) for b in range(-1, NB + 1)}
BEFORE = {-1: 0, 0: BEFORE_FIRST, NB: BEFORE_FULL + (NB - 2) * PER_FULL + len(ORDER[NB - 1])}
BEFORE.update({b: BEFORE_FULL + (b - 1) * PER_FULL for b in range(1, NB)})


def work(b, name, k=0):
    if isinstance(b, int):
        j = BEFORE[b] + ORDER[b].index((name, k))
        return j % 2, j // 2 + 1
    j = BEFORE_FULL - PER_FULL + ORDER[1].index((name, k))
    return j % 2, b * (PER_FULL // 2) + (j // 2 + 1)


def mamba_moe_kernel(nc, x, xT, ctxT, g_xattn, g_ffn, in_wT, conv_w, conv_b, xp_wT, dt_wT, dt_b, A_log, D,
                     gate_wT, wdT, bdT, wuT, bu, ws_dT, bs_d, ws_uT, bs_u, out):
    bc_dram = nc.dram_tensor("bc_scratch", (NB, 2 * NS, L), F32, kind="Internal").ap()
    x2_dram = nc.dram_tensor("x2_scratch", (NB, DM, L), F32, kind="Internal").ap()

    with ExitStack() as ctx:
        def sb(name, shape, dt=F32):
            return ctx.enter_context(nc.sbuf_tensor(name, shape, dt))

        def sem(name):
            return ctx.enter_context(nc.semaphore(name))

        decay = ctx.enter_context(nc.psum_tensor("decay", [P, 2, PAIR, L], F32))
        du = ctx.enter_context(nc.psum_tensor("du", [P, L], F32))
        y = ctx.enter_context(nc.psum_tensor("y", [P, L], F32))
        wk = ctx.enter_context(nc.psum_tensor("wk", [P, 2, L], F32))

        in_w = sb("in_w", [P, KC, DM])
        xp_w = sb("xp_w", [P, NW, R + 2 * NS])
        rows_w = sb("rows_w", [LOW + NE, DM])
        dt_w, b_up = rows_w[0:R, :], rows_w[LOW:LOW + NE, :]
        gate_w = sb("gate_w", [P, NW, NX])
        w_down = sb("w_down", [P, NW, NE, P])
        w_up = sb("w_up", [P, NE, DM])
        conv_taps = sb("conv_taps", [P, NW, TAPS])
        conv_bias = sb("conv_bias", [P, NW])
        dt_bias = sb("dt_bias", [P, NW])
        d_skip = sb("d_skip", [P, NW])
        b_down = sb("b_down", [P, NE])
        a_neg = sb("a_neg", [P, NW, NS])
        gates = sb("gates", [P, 2])
        ident = sb("ident", [P, P])
        mean_w = sb("mean_w", [P, P])
        conv_diag = sb("conv_diag", [P, NW, TAPS, P])
        skip_diag = sb("skip_diag", [P, NW, P])
        expert_no = sb("expert_no", [P, NX])
        consts = sb("consts", [P, 3])
        eps, minus_half, minus_one = (consts[:, k:k + 1] for k in range(3))

        ctx_in = sb("ctx_in", [P, KC, L])
        xpad = sb("xpad", [P, TAPS - 1 + L])
        u = sb("u", [P, NW, L])
        rows_in = sb("rows_in", [LOW + NE, L])
        x_dbl, combT = rows_in[0:R + 2 * NS, :], rows_in[LOW:LOW + NE, :]
        sp_e = sb("sp_e", [P, L])
        sp_w = sb("sp_w", [P, L])
        sp_l = sb("sp_l", [P, L])
        delta = sb("delta", [P, 2, L])
        bc = sb("bc", [P, NG, 2, PAIR, L])
        z = sb("z", [P, 2, L])
        z_stat = sb("z_stat", [P, 6])
        z_mv = sb("z_mv", [P, 2])
        z_ln = sb("z_ln", [P, 4])

        ring = sb("ring", [P, RING, PAIR, L])
        x_res = sb("x_res", [P, L])
        x2 = sb("x2", [P, NW, L])

        xn = sb("xn", [P, NW, L])
        h = sb("h", [P, NE, L])
        logit = sb("logit", [P, NT, NX])
        top = sb("top", [P, NT, NX])
        top_no = sb("top_no", [P, NT, NX], U32)
        top_f = sb("top_f", [P, NT, 2])
        share = sb("share", [P, 4, NT, 1])
        pick = sb("pick", [P, 3, NT, NX])
        x_out = sb("x_out", [P, 2, L])

        ssm_loaded = sem("ssm_loaded")
        ffn_loaded = sem("ffn_loaded")
        pool_consts = sem("pool_consts")
        dve_consts = sem("dve_consts")
        act_consts = sem("act_consts")
        ctx_loaded = sem("ctx_loaded")
        z_loaded = [sem(f"z_loaded{k}") for k in range(2)]
        res_loaded = sem("res_loaded")
        xdbl_stored = sem("xdbl_stored")
        b_loaded = [sem(f"b_loaded{k}") for k in range(NG)]
        c_loaded = [sem(f"c_loaded{k}") for k in range(NG)]
        x2_stored = sem("x2_stored")
        x2_loaded = [sem(f"x2_loaded{k}") for k in range(2)]
        out_stored = [sem(f"out_stored{k}") for k in range(2)]
        filled = [sem(f"filled{k}") for k in range(2)]
        drained = [sem(f"drained{k}") for k in range(2)]
        u_ready = sem("u_ready")
        softplus = sem("softplus")
        sp_fix = sem("sp_fix")
        sp_sum = sem("sp_sum")
        delta_ready = sem("delta_ready")
        du_ready = sem("du_ready")
        exp_ready = sem("exp_ready")
        outer_ready = sem("outer_ready")
        scanned = sem("scanned")
        weighted = sem("weighted")
        summed = sem("summed")
        z_stats = sem("z_stats")
        z_scale = sem("z_scale")
        siluz_ready = sem("siluz_ready")
        gated = sem("gated")
        x2_ready = sem("x2_ready")
        squared = sem("squared")
        rstd_step = sem("rstd_step")
        route_step = sem("route_step")
        route_exp = sem("route_exp")
        gelu_done = sem("gelu_done")

        passed = sem("passed")

        block = ctx.enter_context(nc.Block())
        N_SSM = 9
        N_FFN = 10

        def wait(eng, s, value):
            if not isinstance(value, int) or value > 0:
                eng.wait_ge(s, value)

        def wait_filled(eng, b, name, k=0):
            bank, n = work(b, name, k)
            eng.wait_ge(filled[bank], n)
            return bank

        def wait_drained(eng, b, name, k=0):
            bank, n = work(b, name, k)
            eng.wait_ge(drained[bank], n)

        def apart(eng):
            eng.sem_inc(passed, 1)

        def each_batch(eng, body):
            body(-1)
            body(0)
            with eng.Fori(1, NB - 1) as b:
                body(b)
            body(NB - 1)
            body(NB)

        @block.sync
        def _(sp):
            def load_ctx(m):
                sp.dma_start(ctx_in[:], ctxT[m].rearrange("(k p) l -> p k l", p=P)).then_inc(ctx_loaded, DMA)

            def load_z(bb, c):
                wait(sp, gated, NW * bb + c - 1)
                apart(sp)
                sp.dma_start(z[:, c % 2, :], x[bb, c * P:(c + 1) * P, :]).then_inc(z_loaded[c % 2], DMA)

            def load_bc(m, g):
                wait(sp, outer_ready, GB * (m - 1) + GB - NG + g + 1)
                wait(sp, weighted, GB * (m - 1) + GB - NG + g + 1)
                apart(sp)
                for k, s in ((0, b_loaded[g]), (1, c_loaded[g])):
                    rows = bc_dram[m, k * NS + PAIR * g:k * NS + PAIR * g + PAIR, :].rearrange("n l -> (n l)")
                    sp.dma_start(bc[:, g, k].rearrange("p n l -> p (n l)"),
                                 rows.rearrange("(o f) -> o f", o=1).broadcast_to([P, PAIR * L])).then_inc(s, DMA)

            def reload_x2(m, d):
                wait(sp, x2_stored, DMA * (m + 1))
                wait(sp, out_stored[d % 2], DMA * (2 * m + d // 2))
                apart(sp)
                sp.dma_start(x_out[:, d % 2, :], x2_dram[m, d * P:(d + 1) * P, :]).then_inc(x2_loaded[d % 2], DMA)

            def store_out(b, m, d):
                wait_drained(sp, b, "up", d)
                apart(sp)
                sp.dma_start(out[m, d * P:(d + 1) * P, :], x_out[:, d % 2, :]).then_inc(out_stored[d % 2], DMA)

            load_ctx(0)
            sp.dma_start(in_w[:], in_wT.rearrange("(k p) e -> p k e", p=P)).then_inc(ssm_loaded, DMA)
            sp.dma_start(conv_taps[:], conv_w).then_inc(ssm_loaded, DMA)
            sp.dma_start(conv_bias[:], conv_b).then_inc(ssm_loaded, DMA)
            sp.dma_start(xp_w[:], xp_wT.rearrange("(c p) k -> p c k", p=P)).then_inc(ssm_loaded, DMA)
            sp.dma_start(dt_w, dt_wT).then_inc(ssm_loaded, DMA)
            sp.dma_start(dt_bias[:], dt_b).then_inc(ssm_loaded, DMA)
            sp.dma_start(a_neg[:], A_log).then_inc(ssm_loaded, DMA)
            sp.dma_start(d_skip[:], D).then_inc(ssm_loaded, DMA)
            sp.dma_start(gates[:, 0:1], g_xattn.rearrange("(o f) -> o f", o=1).broadcast_to([P, 1])).then_inc(ssm_loaded, DMA)
            load_z(0, 0)

            def load_ffn_weights():
                sp.dma_start(gates[:, 1:2], g_ffn.rearrange("(o f) -> o f", o=1).broadcast_to([P, 1])).then_inc(ffn_loaded, DMA)
                sp.dma_start(gate_w[:], gate_wT.rearrange("(k p) x -> p k x", p=P)).then_inc(ffn_loaded, DMA)
                sp.dma_start(w_down[:, :, 0:NX, :], wdT.rearrange("(k p) x j -> p k x j", p=P)).then_inc(ffn_loaded, DMA)
                sp.dma_start(w_down[:, :, NX, :], ws_dT.rearrange("(k p) j -> p k j", p=P)).then_inc(ffn_loaded, DMA)
                sp.dma_start(w_up[:, 0:NX, :], wuT).then_inc(ffn_loaded, DMA)
                sp.dma_start(w_up[:, NX, :], ws_uT).then_inc(ffn_loaded, DMA)
                sp.dma_start(b_down[:, 0:NX], bdT).then_inc(ffn_loaded, DMA)
                sp.dma_start(b_down[:, NX:NE], bs_d.rearrange("(p o) -> p o", o=1)).then_inc(ffn_loaded, DMA)
                sp.dma_start(b_up[0:NX, :], bu).then_inc(ffn_loaded, DMA)
                sp.dma_start(b_up[NX:NE, :], bs_u.rearrange("(o d) -> o d", o=1)).then_inc(ffn_loaded, DMA)

            def body(b):
                m = b - 1
                if b_prep(b) and not is_int(b, -1):
                    sp.wait_ge(u_ready, NW * (b + 1))
                    apart(sp)
                    load_ctx(b + 1)
                for c in range(NW):
                    if b_ffn(b) and c == 3:
                        reload_x2(m, 2)
                        store_out(b, m, 1)
                        reload_x2(m, 3)
                    if b_scan(b):
                        if not (is_int(b, NB - 1) and c == NW - 1):
                            load_z(b + (c + 1) // NW, (c + 1) % NW) if c < NW - 1 else load_z(b + 1, 0)
                        wait(sp, x2_ready, NW * b + c)
                        apart(sp)
                        sp.dma_start(x_res[:], xT[b, c * P:(c + 1) * P, :]).then_inc(res_loaded, DMA)
                    if b_ffn(b) and c == 0:
                        wait(sp, x2_ready, NW * (m + 1))
                        apart(sp)
                        sp.dma_start(x2_dram[m].rearrange("(k p) l -> p k l", p=P), x2[:]).then_inc(x2_stored, DMA)
                    if b_ffn(b) and c == 1:
                        reload_x2(m, 0)
                        reload_x2(m, 1)
                    if b_ffn(b) and c == 2:
                        store_out(b, m, 0)
                    if b_prep(b) and c == 3:
                        wait_drained(sp, b, "x_proj")
                        apart(sp)
                        sp.dma_start(bc_dram[b + 1], x_dbl[R:R + 2 * NS, :]).then_inc(xdbl_stored, DMA)
                        sp.wait_ge(xdbl_stored, DMA * (b + 2))
                        for g in range(NG):
                            load_bc(b + 1, g)
                            if b_ffn(b) and g == 3:
                                store_out(b, m, 2)
                            if b_ffn(b) and g == 6:
                                store_out(b, m, 3)
                    elif b_ffn(b) and c == 3:
                        store_out(b, m, 2)
                        store_out(b, m, 3)
                if is_int(b, -1):
                    load_ffn_weights()

            each_batch(sp, body)
            for k in range(2):
                sp.wait_ge(out_stored[k], DMA * 2 * NB)

        @block.gpsimd
        def _(pool):
            made = [0]

            def link(ins):
                made[0] += 1
                ins.then_inc(pool_consts, 1)
                pool.wait_ge(pool_consts, made[0])

            link(nc.gpsimd.memset(ident[:], 0.0))
            link(nc.gpsimd.affine_select(out=ident[:], in_=ident[:], compare_op=ALU.not_equal, fill=1.0, base=0,
                                         pattern=[[-1, P]], channel_multiplier=1))
            link(nc.gpsimd.memset(mean_w[:], 1.0 / DM))
            link(nc.gpsimd.memset(combT, 1.0))
            for k, value in enumerate((EPS, -0.5, -1.0)):
                link(nc.gpsimd.memset(consts[:, k:k + 1], value))
            for k in range(NX):
                link(nc.gpsimd.memset(expert_no[:, k:k + 1], float(k)))
            assert made[0] == POOL_CONSTS

            def softplus_sum(w, par):
                pool.wait_ge(softplus, 3 * w + 3)
                pool.wait_ge(sp_fix, 2 * w + 2)
                nc.gpsimd.tensor_tensor(sp_l[:], sp_l[:], sp_w[:], ALU.add).then_inc(sp_sum, 1)
                pool.wait_ge(sp_sum, w + 1)
                nc.gpsimd.tensor_tensor(delta[:, par, :], delta[:, par, :], sp_l[:], ALU.add).then_inc(delta_ready, 1)

            def z_affine(w):
                pool.wait_ge(z_stats, 2 * w + 2)
                wait(pool, siluz_ready, w)
                nc.gpsimd.tensor_tensor(z_ln[:, 0:1], z_mv[:, 1:2], eps, ALU.add)
                nc.gpsimd.tensor_tensor(z_ln[:, 1:2], z_mv[:, 0:1], minus_one, ALU.mult).then_inc(z_scale, 1)
                pool.wait_ge(z_scale, 3 * w + 1)
                nc.gpsimd.tensor_tensor(z_ln[:, 2:3], z_ln[:, 0:1], minus_half, ALU.pow).then_inc(z_scale, 1)
                pool.wait_ge(z_scale, 3 * w + 2)
                nc.gpsimd.tensor_tensor(z_ln[:, 3:4], z_ln[:, 1:2], z_ln[:, 2:3], ALU.mult).then_inc(z_scale, 1)

            def residual(w, c):
                pool.wait_ge(gated, w + 1)
                pool.wait_ge(res_loaded, DMA * (w + 1))
                nc.gpsimd.tensor_tensor(x2[:, c, :], x2[:, c, :], x_res[:], ALU.add).then_inc(x2_ready, 1)

            def body(b):
                for c in range(NW):
                    w = NW * b + c
                    for g in range(NG):
                        if b_scan(b):
                            i = GB * b + NG * c + g
                            slot = (NG * c + g) % RING
                            if g == 1:
                                z_affine(w)
                            pool.wait_ge(scanned, i + 1)
                            if c == 0:
                                pool.wait_ge(c_loaded[g], DMA * (b + 1))
                            nc.gpsimd.tensor_tensor(ring[:, slot], ring[:, slot], bc[:, g, 1], ALU.mult).then_inc(weighted, 1)
                        if g == 3 and (b_scan(b) and not is_int(b, 0) or is_int(b, 0) and c > 0 or is_int(b, NB) and c == 0):
                            residual(w - 1, (c - 1) % NW)
                        if ("dt", c) in jobs_of_slot(b, c, g):
                            softplus_sum(w + 1, (c + 1) % 2)

            each_batch(pool, body)

        @block.scalar
        def _(act):
            act.wait_ge(ssm_loaded, DMA * N_SSM)
            nc.scalar.activation(a_neg[:], a_neg[:], ACT.Exp).then_inc(act_consts, 1)
            nc.scalar.activation(gates[:, 0:1], gates[:, 0:1], ACT.Tanh).then_inc(act_consts, 1)
            act.wait_ge(pool_consts, POOL_CONSTS)
            act.wait_ge(dve_consts, 2)

            def exps(b, c, g):
                w, i = NW * b + c, GB * b + NG * c + g
                if g == 0:
                    act.wait_ge(delta_ready, w + 1)
                wait(act, scanned, i - 1)
                for n in range(PAIR):
                    last = nc.scalar.activation(decay[:, g % 2, n, 1:L], delta[:, c % 2, 1:L], ACT.Exp,
                                                scale=a_neg[:, c, PAIR * g + n:PAIR * g + n + 1])
                last.then_inc(exp_ready, 1)

            def in_proj_out(b, c):
                bank = wait_filled(act, b, "in_proj", c)
                if not (is_int(b, -1) and c == 0):
                    wait(act, u_ready, NW * (b + 1) + c)
                nc.scalar.activation(xpad[:, TAPS - 1:], wk[:, bank, :], ACT.Copy).then_inc(drained[bank], 1)

            def silu_u(b, c):
                bank = wait_filled(act, b, "conv", c)
                if not is_int(b, -1):
                    act.wait_ge(du_ready, NW * b + c + 1)
                nc.scalar.activation(u[:, c, :], wk[:, bank, :], ACT.Silu, bias=conv_bias[:, c:c + 1]).then_inc(drained[bank], 1)
                wait_drained(act, b, "conv", c)
                act.sem_inc(u_ready, 1)

            def silu_z(b, c):
                w = NW * b + c
                act.wait_ge(z_scale, 3 * w + 3)
                nc.scalar.activation(z[:, c % 2, :], z[:, c % 2, :], ACT.Silu, scale=z_ln[:, 2:3],
                                     bias=z_ln[:, 3:4]).then_inc(siluz_ready, 1)

            def dt_softplus(b, c):
                w, cn = NW * b + c + 1, (c + 1) % NW
                bank = wait_filled(act, b, "dt", c)
                wait(act, sp_fix, 2 * w)
                wait(act, softplus, 3 * w)
                nc.scalar.activation(sp_e[:], wk[:, bank, :], ACT.Abs, bias=dt_bias[:, cn:cn + 1]).then_inc(softplus, 1)
                wait(act, du_ready, w - 1)
                wait(act, exp_ready, NG * (w - 1))
                nc.scalar.activation(delta[:, cn % 2, :], wk[:, bank, :], ACT.Relu, bias=dt_bias[:, cn:cn + 1]).then_inc(drained[bank], 1)
                act.wait_ge(softplus, 3 * w + 1)
                nc.scalar.activation(sp_e[:], sp_e[:], ACT.Exp, scale=-1.0).then_inc(softplus, 1)
                act.wait_ge(softplus, 3 * w + 2)
                wait(act, delta_ready, w)
                nc.scalar.activation(sp_l[:], sp_e[:], ACT.Ln, bias=1.0).then_inc(softplus, 1)

            def jobs_out(b, c, g):
                m = b - 1
                for name, k in jobs_of_slot(b, c, g):
                    if name == "in_proj":
                        in_proj_out(b, c)
                    if name == "conv":
                        silu_u(b, c)
                    if name == "x_proj":
                        bank = wait_filled(act, b, name)
                        wait(act, xdbl_stored, DMA * (b + 1))
                        nc.scalar.activation(x_dbl, wk[0:R + 2 * NS, bank, :], ACT.Copy).then_inc(drained[bank], 1)
                    if name == "dt":
                        dt_softplus(b, c)
                    if name == "mean":
                        wait_drained(act, b, "mean")
                        wait(act, out_stored[(NW - 1) % 2], DMA * 2 * m)
                        nc.scalar.activation(h[:, 0:NW, :], xn[:], ACT.Square).then_inc(squared, 1)
                    if name == "var":
                        bank = wait_filled(act, b, name)
                        nc.scalar.activation(wk[:, bank, :], wk[:, bank, :], ACT.Ln, bias=eps).then_inc(rstd_step, 1)
                        act.wait_ge(rstd_step, 2 * m + 1)
                        nc.scalar.activation(wk[:, bank, :], wk[:, bank, :], ACT.Exp, scale=-0.5).then_inc(rstd_step, 1)
                    if name == "logits":
                        act.wait_ge(route_step, ROUTE_STEPS * m + 4)
                        nc.scalar.activation(share[:, 1], share[:, 0], ACT.Exp).then_inc(route_exp, 1)
                    if name == "comb":
                        bank = wait_filled(act, b, name)
                        nc.scalar.activation(combT[0:NX, :], wk[0:NX, bank, :], ACT.Copy).then_inc(drained[bank], 1)
                    if name == "down":
                        bank = wait_filled(act, b, name, k)
                        nc.scalar.activation(h[:, k, :], wk[:, bank, :], ACT.Identity, bias=b_down[:, k:k + 1]).then_inc(drained[bank], 1)
                        if k % GELU_EVERY == GELU_EVERY - 1:
                            for j in range(k - 1, k + 1):
                                wait_drained(act, b, name, j)
                            nc.scalar.activation(h[:, k - GELU_EVERY + 1:k + 1, :], h[:, k - GELU_EVERY + 1:k + 1, :],
                                                 ACT.Gelu).then_inc(gelu_done, 1)

            def body(b):
                if is_int(b, 0):
                    act.wait_ge(ffn_loaded, DMA * N_FFN)
                    nc.scalar.activation(gates[:, 1:2], gates[:, 1:2], ACT.Tanh).then_inc(act_consts, 1)
                for c in range(NW):
                    for g in range(NG):
                        if b_scan(b):
                            if g < NG - 1:
                                exps(b, c, g + 1)
                            elif c < NW - 1:
                                exps(b, c + 1, 0)
                            elif not is_int(b, NB - 1):
                                exps(b + 1, 0, 0)
                        jobs_out(b, c, g)
                        if b_scan(b) and g == 3:
                            silu_z(b, c)
                if is_int(b, -1):
                    exps(0, 0, 0)

            each_batch(act, body)

        @block.vector
        def _(dve):
            nc.vector.memset(xpad[:, 0:TAPS - 1], 0.0)
            nc.vector.memset(decay[:, :, :, 0:1], 0.0).then_inc(dve_consts, 1)
            dve.wait_ge(act_consts, 1)
            nc.vector.tensor_scalar(a_neg[:], a_neg[:], -1.0, None, ALU.mult).then_inc(dve_consts, 1)
            dve.wait_ge(ssm_loaded, DMA * N_SSM)
            dve.wait_ge(pool_consts, POOL_CONSTS)
            for c in range(NW):
                for k in range(TAPS):
                    nc.vector.tensor_scalar(conv_diag[:, c, k, :], ident[:], conv_taps[:, c, k:k + 1], None, ALU.mult)
                last = nc.vector.tensor_scalar(skip_diag[:, c, :], ident[:], d_skip[:, c:c + 1], None, ALU.mult)
            last.then_inc(dve_consts, 1)

            def delta_u(b, c):
                w = NW * b + c
                dve.wait_ge(delta_ready, w + 1)
                dve.wait_ge(u_ready, w + 1)
                wait(dve, outer_ready, NG * w)
                nc.vector.tensor_tensor(du[:], delta[:, c % 2, :], u[:, c, :], ALU.mult).then_inc(du_ready, 1)
                dve.wait_ge(du_ready, w + 1)

            def group(b, c, g):
                i = GB * b + NG * c + g
                slot = (NG * c + g) % RING
                if c == 0:
                    dve.wait_ge(b_loaded[g], DMA * (b + 1))
                wait(dve, summed, i + 1 - RING)
                nc.vector.tensor_tensor(ring[:, slot], du[:, None, :].broadcast_to([P, PAIR, L]), bc[:, g, 0],
                                        ALU.mult).then_inc(outer_ready, 1)
                dve.wait_ge(outer_ready, i + 1)
                dve.wait_ge(exp_ready, i + 1)
                states = ring[:, slot].rearrange("p n l -> p (n l)")
                nc.vector.tensor_tensor_scan(states, decay[:, g % 2].rearrange("p n l -> p (n l)"), states, 0.0,
                                             ALU.mult, ALU.add).then_inc(scanned, 1)

            def stats_z(b, c):
                w = NW * b + c
                dve.wait_ge(z_loaded[c % 2], DMA * (2 * b + c // 2 + 1))
                wait(dve, z_scale, 3 * w)
                nc.vector.bn_stats(z_stat[:], z[:, c % 2, :]).then_inc(z_stats, 1)
                dve.wait_ge(z_stats, 2 * w + 1)
                apart(dve)
                nc.vector.bn_aggr(z_mv[:], z_stat[:]).then_inc(z_stats, 1)

            def gate(b, c):
                w = NW * b + c
                dve.wait_ge(summed, NG * (w + 1))
                dve.wait_ge(siluz_ready, w + 1)
                if not is_int(b, 0):
                    dve.wait_ge(x2_stored, DMA * b)
                nc.vector.scalar_tensor_tensor(x2[:, c, :], y[:], gates[:, 0:1], z[:, c % 2, :], ALU.mult,
                                               ALU.mult).then_inc(gated, 1)

            def softplus_fix(b, c):
                w = NW * b + c + 1
                dve.wait_ge(softplus, 3 * w + 2)
                wait(dve, delta_ready, w)
                nc.vector.tensor_scalar(sp_w[:], sp_e[:], 1.0, -1.0, ALU.add, ALU.add).then_inc(sp_fix, 1)
                dve.wait_ge(sp_fix, 2 * w + 1)
                nc.vector.scalar_tensor_tensor(sp_w[:], sp_w[:], -1.0, sp_e[:], ALU.mult, ALU.add).then_inc(sp_fix, 1)

            def centre(b):
                bank = wait_filled(dve, b, "mean")
                nc.vector.tensor_tensor(xn[:], x2[:], wk[:, bank, None, :].broadcast_to([P, NW, L]),
                                        ALU.subtract).then_inc(drained[bank], 1)
                wait_drained(dve, b, "mean")

            def normalise(b):
                m = b - 1
                bank, _ = work(b, "var")
                dve.wait_ge(rstd_step, 2 * m + 2)
                dve.wait_ge(squared, m + 1)
                nc.vector.tensor_tensor(xn[:], xn[:], wk[:, bank, None, :].broadcast_to([P, NW, L]),
                                        ALU.mult).then_inc(drained[bank], 1)

            def route(b):
                m = b - 1
                steps = [0]

                def link(ins):
                    steps[0] += 1
                    ins.then_inc(route_step, 1)
                    dve.wait_ge(route_step, ROUTE_STEPS * m + steps[0])

                def over_experts(t):
                    return t.broadcast_to([P, NT, NX])

                bank = wait_filled(dve, b, "logits")
                nc.vector.tensor_copy(logit[:].rearrange("p t x -> p (t x)"), wk[:, bank, 0:NT * NX]).then_inc(drained[bank], 1)
                wait_drained(dve, b, "logits")
                apart(dve)
                for t in range(NT):
                    last = nc.vector.max(top[:, t, :], logit[:, t, :])
                link(last)
                apart(dve)
                for t in range(NT):
                    last = nc.vector.max_index(top_no[:, t, :], top[:, t, :], logit[:, t, :])
                link(last)
                link(nc.vector.tensor_copy(top_f[:], top_no[:, :, 0:2]))
                link(nc.vector.tensor_tensor(share[:, 0], top[:, :, 1:2], top[:, :, 0:1], ALU.subtract))
                numbers = expert_no[:, None, :].broadcast_to([P, NT, NX])
                link(nc.vector.tensor_tensor(pick[:, 0], numbers, over_experts(top_f[:, :, 0:1]), ALU.is_equal))
                link(nc.vector.tensor_tensor(pick[:, 1], numbers, over_experts(top_f[:, :, 1:2]), ALU.is_equal))
                dve.wait_ge(route_exp, m + 1)
                link(nc.vector.tensor_scalar(share[:, 2], share[:, 1], 1.0, None, ALU.add))
                link(nc.vector.reciprocal(share[:, 2], share[:, 2]))
                link(nc.vector.tensor_tensor(share[:, 3], share[:, 1], share[:, 2], ALU.mult))
                link(nc.vector.tensor_tensor(pick[:, 0], pick[:, 0], over_experts(share[:, 2]), ALU.mult))
                link(nc.vector.tensor_tensor(pick[:, 1], pick[:, 1], over_experts(share[:, 3]), ALU.mult))
                link(nc.vector.tensor_tensor(pick[:, 2], pick[:, 0], pick[:, 1], ALU.add))
                link(nc.vector.tensor_copy(top_f[:, :, 0:1], share[:, 0]))
                assert steps[0] == ROUTE_STEPS

            def mix(b, k):
                m = b - 1
                bank = wait_filled(dve, b, "mix", k)
                dve.wait_ge(gelu_done, NE // GELU_EVERY * m + k // GELU_EVERY + 1)
                nc.vector.tensor_tensor(h[:, k, :], h[:, k, :], wk[:, bank, :], ALU.mult).then_inc(drained[bank], 1)

            def up_out(b, d):
                m = b - 1
                bank = wait_filled(dve, b, "up", d)
                dve.wait_ge(x2_loaded[d % 2], DMA * (2 * m + d // 2 + 1))
                nc.vector.scalar_tensor_tensor(x_out[:, d % 2, :], wk[:, bank, :], gates[:, 1:2], x_out[:, d % 2, :],
                                               ALU.mult, ALU.add).then_inc(drained[bank], 1)

            def body(b):
                for c in range(NW):
                    for g in range(NG):
                        if g == 2 and (b_scan(b) and not is_int(b, 0) or is_int(b, 0) and c > 0 or is_int(b, NB) and c == 0):
                            if c == 0:
                                gate(b - 1, NW - 1)
                            else:
                                gate(b, c - 1)
                        if b_scan(b):
                            if g == 0:
                                delta_u(b, c)
                            group(b, c, g)
                            if g == 0:
                                stats_z(b, c)
                        for name, k in jobs_of_slot(b, c, g):
                            if name == "dt":
                                softplus_fix(b, c)
                            if name == "mean":
                                centre(b)
                            if name == "var":
                                normalise(b)
                            if name == "logits":
                                route(b)
                            if name == "mix":
                                mix(b, k)
                            if name == "up":
                                up_out(b, k)
                if is_int(b, 0):
                    dve.wait_ge(act_consts, 3)

            dve.wait_ge(act_consts, 2)
            each_batch(dve, body)

        @block.tensor
        def _(pe):
            pe.wait_ge(ssm_loaded, DMA * N_SSM)
            pe.wait_ge(pool_consts, POOL_CONSTS)
            pe.wait_ge(dve_consts, 3)

            def sum_group(b, c, g):
                w, i = NW * b + c, GB * b + NG * c + g
                slot = (NG * c + g) % RING
                if g == 0:
                    wait(pe, gated, w)
                    pe.wait_ge(u_ready, w + 1)
                    nc.tensor.matmul(y[:], skip_diag[:, c, :], u[:, c, :], start=True, stop=False)
                pe.wait_ge(weighted, i + 1)
                for n in range(PAIR):
                    last = nc.tensor.matmul(y[:], ident[:], ring[:, slot, n, :], start=False,
                                            stop=(g == NG - 1 and n == PAIR - 1))
                last.then_inc(summed, 1)

            def job(b, name, k):
                m = b - 1
                bank, n = work(b, name, k)
                wait(pe, drained[bank], n - 1)
                o = wk[:, bank, :]
                if name == "in_proj":
                    if k == 0:
                        pe.wait_ge(ctx_loaded, DMA * (b + 2))
                    for j in range(KC):
                        last = nc.tensor.matmul(o, in_w[:, j, k * P:(k + 1) * P], ctx_in[:, j, :], start=j == 0, stop=j == KC - 1)
                if name == "conv":
                    wait_drained(pe, b, "in_proj", k)
                    for j in range(TAPS):
                        last = nc.tensor.matmul(o, conv_diag[:, k, j, :], xpad[:, j:j + L], start=j == 0, stop=j == TAPS - 1)
                if name == "x_proj":
                    pe.wait_ge(u_ready, NW * (b + 2))
                    for j in range(NW):
                        last = nc.tensor.matmul(o[0:R + 2 * NS, :], xp_w[:, j, :], u[:, j, :], start=j == 0, stop=j == NW - 1)
                if name == "dt":
                    if k == NW - 1:
                        wait_drained(pe, b, "x_proj")
                    kn = (k + 1) % NW
                    last = nc.tensor.matmul(o, dt_w[:, kn * P:(kn + 1) * P], x_dbl[0:R, :], start=True, stop=True)
                if name == "mean":
                    pe.wait_ge(x2_ready, NW * b)
                    for j in range(NW):
                        last = nc.tensor.matmul(o, mean_w[:], x2[:, j, :], start=j == 0, stop=j == NW - 1)
                if name == "var":
                    pe.wait_ge(squared, m + 1)
                    for j in range(NW):
                        last = nc.tensor.matmul(o, mean_w[:], h[:, j, :], start=j == 0, stop=j == NW - 1)
                if name == "logits":
                    wait_drained(pe, b, "var")
                    for t in range(NT):
                        for j in range(NW):
                            last = nc.tensor.matmul(o[:, t * NX:(t + 1) * NX], xn[:, j, t * P:(t + 1) * P], gate_w[:, j, :],
                                                    start=j == 0, stop=j == NW - 1)
                if name == "comb":
                    pe.wait_ge(route_step, ROUTE_STEPS * b)
                    for t in range(NT):
                        last = nc.tensor.transpose(o[0:NX, t * P:(t + 1) * P], pick[:, 2, t, :], ident[:])
                if name == "down":
                    for j in range(NW):
                        last = nc.tensor.matmul(o, w_down[:, j, k, :], xn[:, j, :], start=j == 0, stop=j == NW - 1)
                if name == "mix":
                    if k == 0:
                        wait_drained(pe, b, "comb")
                    last = nc.tensor.matmul(o, ident[LOW:LOW + NX, LOW + k:LOW + k + 1].broadcast_to([NX, P]), combT[0:NX, :], start=True, stop=True)
                if name == "up":
                    if k == 0:
                        for j in range(NX - 2, NX):
                            wait_drained(pe, b, "mix", j)
                        pe.wait_ge(gelu_done, NE // GELU_EVERY * b)
                    for j in range(NE):
                        nc.tensor.matmul(o, w_up[:, j, k * P:(k + 1) * P], h[:, j, :], start=j == 0, stop=False)
                    last = nc.tensor.matmul(o, b_up[:, k * P:(k + 1) * P], combT, start=False, stop=True)
                last.then_inc(filled[bank], 1)

            def body(b):
                for c in range(NW):
                    for g in range(NG):
                        k = NG * c + g - LAG
                        if k >= 0 and b_scan(b):
                            sum_group(b, k // NG, k % NG)
                        elif k < 0 and not (isinstance(b, int) and b <= 0):
                            sum_group(b - 1, NW - 1, NG + k)
                        for name, j in jobs_of_slot(b, c, g):
                            job(b, name, j)
                if is_int(b, 0):
                    pe.wait_ge(ffn_loaded, DMA * N_FFN)

            each_batch(pe, body)


_INS = ['x', 'xT', 'ctxT', 'g_xattn', 'g_ffn', 'in_wT', 'conv_w', 'conv_b', 'xp_wT', 'dt_wT', 'dt_b', 'A_log', 'D',
        'gate_wT', 'wdT', 'bdT', 'wuT', 'bu', 'ws_dT', 'bs_d', 'ws_uT', 'bs_u']


def kernel(x, ctx_1024, g_xattn, g_ffn, L0_xattn_in_proj_w, L0_xattn_conv_w, L0_xattn_conv_b, L0_xattn_x_proj_w,
           L0_xattn_dt_proj_w, L0_xattn_dt_proj_b, L0_xattn_A_log, L0_xattn_D, L0_ffn_gate_w, L0_ffn_wd, L0_ffn_bd,
           L0_ffn_wu, L0_ffn_bu, L0_ffn_ws_d, L0_ffn_bs_d, L0_ffn_ws_u, L0_ffn_bs_u):
    import numpy as np
    import concourse.bacc as bacc
    from concourse.bass_utils import run_bass_kernel_spmd

    def by_partition(t):
        t = np.asarray(t)
        return np.swapaxes(t.reshape((NW, P) + t.shape[1:]), 0, 1)

    laid = {
        'x': x, 'xT': np.transpose(x, (0, 2, 1)), 'ctxT': np.transpose(ctx_1024, (0, 2, 1)),
        'g_xattn': g_xattn, 'g_ffn': g_ffn, 'in_wT': np.transpose(L0_xattn_in_proj_w),
        'conv_w': by_partition(L0_xattn_conv_w), 'conv_b': by_partition(L0_xattn_conv_b), 'xp_wT': np.transpose(L0_xattn_x_proj_w),
        'dt_wT': np.transpose(L0_xattn_dt_proj_w), 'dt_b': by_partition(L0_xattn_dt_proj_b), 'A_log': by_partition(L0_xattn_A_log),
        'D': by_partition(L0_xattn_D), 'gate_wT': np.transpose(L0_ffn_gate_w), 'wdT': np.transpose(L0_ffn_wd, (2, 0, 1)),
        'bdT': np.transpose(L0_ffn_bd), 'wuT': np.transpose(L0_ffn_wu, (2, 0, 1)), 'bu': L0_ffn_bu,
        'ws_dT': np.transpose(L0_ffn_ws_d), 'bs_d': L0_ffn_bs_d, 'ws_uT': np.transpose(L0_ffn_ws_u),
        'bs_u': L0_ffn_bs_u,
    }
    nc = bacc.Bacc("TRN2", target_bir_lowering=False, num_devices=1)
    arrays, args = {}, []
    for name in _INS:
        a = np.ascontiguousarray(laid[name])
        arrays[f"in_{name}"] = a
        args.append(nc.dram_tensor(f"in_{name}", a.shape, mybir.dt.from_np(a.dtype), kind="ExternalInput").ap())
    out = nc.dram_tensor("out_T", (NB, DM, L), F32, kind="ExternalOutput").ap()
    mamba_moe_kernel(nc, *args, out)
    r = run_bass_kernel_spmd(nc, [arrays], core_ids=[0])
    return np.ascontiguousarray(np.transpose(r.results[0]["out_T"], (0, 2, 1)))
```

```python
from contextlib import ExitStack

import concourse.bass as bass
from concourse import mybir

ALU = mybir.AluOpType
ACT = mybir.ActivationFunctionType
F32 = mybir.dt.float32
BF16 = mybir.dt.bfloat16
U32 = mybir.dt.uint32

P = 128
NB = 4
L = 512
DM = 512
DCTX = 256
KC = DCTX // P
NW = DM // P
NS = 16
PAIR = 2
NG = NS // PAIR
GB = NW * NG
R = 16
TAPS = 4
NX = 8
NE = NX + 1
NT = L // P
RING = 4
LAG = 2
LOW = 64
EPS = 1e-5
DMA = 16
PARTS = 3
NC = PARTS * NX
POOL_CONSTS = 8 + PARTS + NX
ROUTE_STEPS = 19


PREP_JOBS = {
    (0, 1): [("in_proj", 0)], (1, 1): [("in_proj", 1)], (2, 1): [("in_proj", 2)], (2, 5): [("in_proj", 3)],
    (3, 1): [("x_proj", 0)],
}
CONVS = {(0, 3): 0, (1, 3): 1, (2, 3): 2, (2, 6): 3}
SILUS = {(0, 4): 0, (1, 4): 1, (2, 4): 2, (2, 7): 3}
DT_GROUP = 3
FFN_JOBS = {
    (0, 3): [("mean", 0)], (0, 6): [("var", 0)],
    (1, 0): [("logits", 0), ("down", 0)], (1, 1): [("down", 1)], (1, 2): [("down", 2)], (1, 3): [("down", 3), ("comb", 0)],
    (1, 4): [("down", 4)], (1, 5): [("down", 5), ("mix", 0)], (1, 6): [("down", 6), ("mix", 1)],
    (1, 7): [("down", 7), ("mix", 2)], (2, 0): [("down", 8), ("mix", 3)], (2, 1): [("mix", 4)],
    (2, 2): [("mix", 5), ("mix", 6)], (2, 3): [("mix", 7)],
    (2, 4): [("up", 0)], (2, 7): [("up", 1)], (3, 2): [("up", 2)], (3, 5): [("up", 3)],
}
UP_STARTS = {(2, 3): 0, (2, 6): 1, (3, 0): 2, (3, 4): 3}
UP_SPLIT = 4
GELUS = [((1, 4), 0, UP_SPLIT), ((2, 1), UP_SPLIT, NE)]
SQUARE_SLOT = (0, 5)


def jobs_of_slot(b, c, g):
    jobs = []
    if g == DT_GROUP and (b_scan(b) or c == NW - 1) and not is_int(b, NB) and not (is_int(b, NB - 1) and c == NW - 1):
        jobs.append(("dt", c))
    if b_prep(b):
        jobs += PREP_JOBS.get((c, g), [])
    if b_ffn(b):
        jobs += FFN_JOBS.get((c, g), [])
    return jobs


def outs_of_slot(b, c, g, later=1):
    k = NG * c + g - later
    return jobs_of_slot(b, k // NG, k % NG) if k >= 0 else []


def is_int(b, value):
    return isinstance(b, int) and b == value


def b_prep(b):
    return not (isinstance(b, int) and b >= NB - 1)


def b_ffn(b):
    return not (isinstance(b, int) and b <= 0)


def b_scan(b):
    return not (isinstance(b, int) and (b < 0 or b == NB))


def jobs_of_body(b):
    return [j for c in range(NW) for g in range(NG) for j in jobs_of_slot(b, c, g)]


BEFORE_FIRST = len(jobs_of_body(-1))
BEFORE_FULL = BEFORE_FIRST + len(jobs_of_body(0))
PER_FULL = len(jobs_of_body(1))
assert PER_FULL % 2 == 0
ORDER = {b: jobs_of_body(b) for b in range(-1, NB + 1)}
BEFORE = {-1: 0, 0: BEFORE_FIRST, NB: BEFORE_FULL + (NB - 2) * PER_FULL + len(ORDER[NB - 1])}
BEFORE.update({b: BEFORE_FULL + (b - 1) * PER_FULL for b in range(1, NB)})


def work(b, name, k=0):
    if isinstance(b, int):
        j = BEFORE[b] + ORDER[b].index((name, k))
        return j % 2, j // 2 + 1
    j = BEFORE_FULL - PER_FULL + ORDER[1].index((name, k))
    return j % 2, b * (PER_FULL // 2) + (j // 2 + 1)


def mamba_moe_kernel(nc, x, xT, ctxT, g_xattn, g_ffn, in_wT, conv_w, conv_b, xp_wT, dt_wT, dt_b, A_log, D,
                     gate_wT, wdT, bdT, wuT, bu, ws_dT, bs_d, ws_uT, bs_u, out):
    bc_dram = nc.dram_tensor("bc_scratch", (NB, 2 * NS, L), F32, kind="Internal").ap()
    x2_dram = nc.dram_tensor("x2_scratch", (NB, DM, L), F32, kind="Internal").ap()

    with ExitStack() as ctx:
        def sb(name, shape, dt=F32):
            return ctx.enter_context(nc.sbuf_tensor(name, shape, dt))

        def sem(name):
            return ctx.enter_context(nc.semaphore(name))

        decay = ctx.enter_context(nc.psum_tensor("decay", [P, 2, PAIR, L], F32))
        du = ctx.enter_context(nc.psum_tensor("du", [P, L], F32))
        y = ctx.enter_context(nc.psum_tensor("y", [P, L], F32))
        wk = ctx.enter_context(nc.psum_tensor("wk", [P, 2, L], F32))

        in_w = sb("in_w", [P, KC, DM])
        xp_w = sb("xp_w", [P, NW, R + 2 * NS])
        rows_w = sb("rows_w", [LOW + NC + 1, DM])
        dt_w, b_up = rows_w[0:R, :], rows_w[LOW:LOW + NC + 1, :]
        gate_w = sb("gate_w", [P, NW, NX])
        w_down = sb("w_down", [P, NW, NE, P])
        w_up = sb("w_up", [P, NE, DM])
        conv_taps = sb("conv_taps", [P, NW, TAPS])
        conv_bias = sb("conv_bias", [P, NW])
        dt_bias = sb("dt_bias", [P, NW])
        d_skip = sb("d_skip", [P, NW])
        b_down = sb("b_down", [P, NE])
        a_neg = sb("a_neg", [P, NW, NS])
        gates = sb("gates", [P, 2])
        ident = sb("ident", [P, P])
        mean_w = sb("mean_w", [P, P])
        sel = sb("sel", [NC, NX], BF16)
        expert_no = sb("expert_no", [P, NX])
        consts = sb("consts", [P, 3])
        eps, minus_half, minus_one = (consts[:, k:k + 1] for k in range(3))

        ctx_in = sb("ctx_in", [P, KC, L])
        xpad = sb("xpad", [P, TAPS - 1 + L])
        u = sb("u", [P, NW + 1, L])
        rows_in = sb("rows_in", [LOW + NC + 1, L])
        x_dbl, combT = rows_in[0:R + 2 * NS, :], rows_in[LOW:LOW + NC + 1, :]
        comb_parts = sb("comb_parts", [NC, L], BF16)
        sp_e = sb("sp_e", [P, L])
        sp_w = sb("sp_w", [P, L])
        sp_l = sb("sp_l", [P, L])
        delta = sb("delta", [P, 2, L])
        bc = sb("bc", [P, NG, 2, PAIR, L])
        z = sb("z", [P, 2, L])
        z_stat = sb("z_stat", [P, 6])
        z_mv = sb("z_mv", [P, 2])
        z_ln = sb("z_ln", [P, 4])

        ring = sb("ring", [P, RING, PAIR, L])
        x_res = sb("x_res", [P, L])
        x2 = sb("x2", [P, NW, L])

        xn = sb("xn", [P, NW, L])
        h = sb("h", [P, NE, L])
        logit = sb("logit", [P, NT, NX])
        top = sb("top", [P, NT, NX])
        top_no = sb("top_no", [P, NT, NX], U32)
        top_f = sb("top_f", [P, NT, 2])
        share = sb("share", [P, 4, NT, 1])
        pick = sb("pick", [P, 3, NT, NX])
        part16 = sb("part16", [P, NT, NX], BF16)
        parts = sb("parts", [P, NT, PARTS, NX])
        x_out = sb("x_out", [P, 2, L])

        ssm_loaded = sem("ssm_loaded")
        ffn_loaded = sem("ffn_loaded")
        pool_consts = sem("pool_consts")
        dve_consts = sem("dve_consts")
        act_consts = sem("act_consts")
        ctx_loaded = sem("ctx_loaded")
        z_loaded = [sem(f"z_loaded{k}") for k in range(2)]
        res_loaded = sem("res_loaded")
        u_copied = sem("u_copied")
        xdbl_stored = sem("xdbl_stored")
        b_loaded = [sem(f"b_loaded{k}") for k in range(NG)]
        c_loaded = [sem(f"c_loaded{k}") for k in range(NG)]
        x2_stored = sem("x2_stored")
        x2_loaded = [sem(f"x2_loaded{k}") for k in range(2)]
        out_stored = [sem(f"out_stored{k}") for k in range(2)]
        filled = [sem(f"filled{k}") for k in range(2)]
        drained = [sem(f"drained{k}") for k in range(2)]
        u_ready = sem("u_ready")
        softplus = sem("softplus")
        sp_fix = sem("sp_fix")
        sp_sum = sem("sp_sum")
        delta_ready = sem("delta_ready")
        du_ready = sem("du_ready")
        exp_ready = sem("exp_ready")
        outer_ready = sem("outer_ready")
        scanned = sem("scanned")
        weighted = sem("weighted")
        skipped = sem("skipped")
        paired = sem("paired")
        summed = sem("summed")
        conv_step = sem("conv_step")
        z_stats = sem("z_stats")
        z_scale = sem("z_scale")
        siluz_ready = sem("siluz_ready")
        gated = sem("gated")
        x2_ready = sem("x2_ready")
        squared = sem("squared")
        rstd_step = sem("rstd_step")
        route_step = sem("route_step")
        route_exp = sem("route_exp")
        gelu_done = sem("gelu_done")

        passed = sem("passed")

        block = ctx.enter_context(nc.Block())
        N_SSM = 9
        N_FFN = 9 + PARTS

        def wait(eng, s, value):
            if not isinstance(value, int) or value > 0:
                eng.wait_ge(s, value)

        def wait_filled(eng, b, name, k=0):
            bank, n = work(b, name, k)
            eng.wait_ge(filled[bank], n)
            return bank

        def wait_drained(eng, b, name, k=0):
            bank, n = work(b, name, k)
            eng.wait_ge(drained[bank], n)

        def apart(eng):
            eng.sem_inc(passed, 1)

        def u_place(c):
            return NW if c == NW - 1 else c

        def u_there(eng, b, c):
            if c == NW - 1:
                eng.wait_ge(u_copied, DMA * (b + 1))
            else:
                eng.wait_ge(u_ready, NW * b + c + 1)

        def each_batch(eng, body):
            body(-1)
            body(0)
            with eng.Fori(1, NB - 1) as b:
                body(b)
            body(NB - 1)
            body(NB)

        @block.sync
        def _(sp):
            def load_ctx(m):
                sp.dma_start(ctx_in[:], ctxT[m].rearrange("(k p) l -> p k l", p=P)).then_inc(ctx_loaded, DMA)

            def load_z(bb, c):
                wait(sp, gated, NW * bb + c - 1)
                apart(sp)
                sp.dma_start(z[:, c % 2, :], x[bb, c * P:(c + 1) * P, :]).then_inc(z_loaded[c % 2], DMA)

            def load_bc(m, g):
                wait(sp, outer_ready, GB * (m - 1) + GB - NG + g + 1)
                wait(sp, weighted, GB * (m - 1) + GB - NG + g + 1)
                apart(sp)
                for k, s in ((0, b_loaded[g]), (1, c_loaded[g])):
                    rows = bc_dram[m, k * NS + PAIR * g:k * NS + PAIR * g + PAIR, :].rearrange("n l -> (n l)")
                    sp.dma_start(bc[:, g, k].rearrange("p n l -> p (n l)"),
                                 rows.rearrange("(o f) -> o f", o=1).broadcast_to([P, PAIR * L])).then_inc(s, DMA)

            def reload_x2(m, d):
                wait(sp, x2_stored, DMA * (m + 1))
                wait(sp, out_stored[d % 2], DMA * (2 * m + d // 2))
                apart(sp)
                sp.dma_start(x_out[:, d % 2, :], x2_dram[m, d * P:(d + 1) * P, :]).then_inc(x2_loaded[d % 2], DMA)

            def store_out(b, m, d):
                wait_drained(sp, b, "up", d)
                apart(sp)
                sp.dma_start(out[m, d * P:(d + 1) * P, :], x_out[:, d % 2, :]).then_inc(out_stored[d % 2], DMA)

            load_ctx(0)
            sp.dma_start(in_w[:], in_wT.rearrange("(k p) e -> p k e", p=P)).then_inc(ssm_loaded, DMA)
            sp.dma_start(conv_taps[:], conv_w).then_inc(ssm_loaded, DMA)
            sp.dma_start(conv_bias[:], conv_b).then_inc(ssm_loaded, DMA)
            sp.dma_start(xp_w[:], xp_wT.rearrange("(c p) k -> p c k", p=P)).then_inc(ssm_loaded, DMA)
            sp.dma_start(dt_w, dt_wT).then_inc(ssm_loaded, DMA)
            sp.dma_start(dt_bias[:], dt_b).then_inc(ssm_loaded, DMA)
            sp.dma_start(a_neg[:], A_log).then_inc(ssm_loaded, DMA)
            sp.dma_start(d_skip[:], D).then_inc(ssm_loaded, DMA)
            sp.dma_start(gates[:, 0:1], g_xattn.rearrange("(o f) -> o f", o=1).broadcast_to([P, 1])).then_inc(ssm_loaded, DMA)
            load_z(0, 0)

            def load_ffn_weights():
                sp.dma_start(gates[:, 1:2], g_ffn.rearrange("(o f) -> o f", o=1).broadcast_to([P, 1])).then_inc(ffn_loaded, DMA)
                sp.dma_start(gate_w[:], gate_wT.rearrange("(k p) x -> p k x", p=P)).then_inc(ffn_loaded, DMA)
                sp.dma_start(w_down[:, :, 0:NX, :], wdT.rearrange("(k p) x j -> p k x j", p=P)).then_inc(ffn_loaded, DMA)
                sp.dma_start(w_down[:, :, NX, :], ws_dT.rearrange("(k p) j -> p k j", p=P)).then_inc(ffn_loaded, DMA)
                sp.dma_start(w_up[:, 0:NX, :], wuT).then_inc(ffn_loaded, DMA)
                sp.dma_start(w_up[:, NX, :], ws_uT).then_inc(ffn_loaded, DMA)
                sp.dma_start(b_down[:, 0:NX], bdT).then_inc(ffn_loaded, DMA)
                sp.dma_start(b_down[:, NX:NE], bs_d.rearrange("(p o) -> p o", o=1)).then_inc(ffn_loaded, DMA)
                for k in range(PARTS):
                    sp.dma_start(b_up[k * NX:(k + 1) * NX, :], bu).then_inc(ffn_loaded, DMA)
                sp.dma_start(b_up[NC:NC + 1, :], bs_u.rearrange("(o d) -> o d", o=1)).then_inc(ffn_loaded, DMA)

            def copy_u(b):
                wait(sp, gated, NW * b)
                sp.wait_ge(u_ready, NW * (b + 1))
                apart(sp)
                sp.dma_start(u[:, NW, :], u[:, NW - 1, :]).then_inc(u_copied, DMA)

            def body(b):
                m = b - 1
                if b_prep(b) and not is_int(b, -1):
                    sp.wait_ge(u_ready, NW * (b + 1))
                    apart(sp)
                    load_ctx(b + 1)
                for c in range(NW):
                    if b_scan(b) and c == 1:
                        copy_u(b)
                    if b_ffn(b) and c == 3:
                        reload_x2(m, 2)
                        store_out(b, m, 1)
                        reload_x2(m, 3)
                    if b_scan(b):
                        if not (is_int(b, NB - 1) and c == NW - 1):
                            load_z(b + (c + 1) // NW, (c + 1) % NW) if c < NW - 1 else load_z(b + 1, 0)
                        wait(sp, x2_ready, NW * b + c)
                        apart(sp)
                        sp.dma_start(x_res[:], xT[b, c * P:(c + 1) * P, :]).then_inc(res_loaded, DMA)
                    if b_ffn(b) and c == 0:
                        wait(sp, x2_ready, NW * (m + 1))
                        apart(sp)
                        sp.dma_start(x2_dram[m].rearrange("(k p) l -> p k l", p=P), x2[:]).then_inc(x2_stored, DMA)
                    if b_ffn(b) and c == 1:
                        reload_x2(m, 0)
                        reload_x2(m, 1)
                    if b_ffn(b) and c == 2:
                        store_out(b, m, 0)
                    if b_prep(b) and c == 3:
                        wait_drained(sp, b, "x_proj")
                        apart(sp)
                        sp.dma_start(bc_dram[b + 1], x_dbl[R:R + 2 * NS, :]).then_inc(xdbl_stored, DMA)
                        sp.wait_ge(xdbl_stored, DMA * (b + 2))
                        for g in range(NG):
                            load_bc(b + 1, g)
                            if b_ffn(b) and g == 3:
                                store_out(b, m, 2)
                            if b_ffn(b) and g == 6:
                                store_out(b, m, 3)
                    elif b_ffn(b) and c == 3:
                        store_out(b, m, 2)
                        store_out(b, m, 3)
                if is_int(b, -1):
                    load_ffn_weights()

            each_batch(sp, body)
            for k in range(2):
                sp.wait_ge(out_stored[k], DMA * 2 * NB)

        @block.gpsimd
        def _(pool):
            made = [0]

            def link(ins):
                made[0] += 1
                ins.then_inc(pool_consts, 1)
                pool.wait_ge(pool_consts, made[0])

            link(nc.gpsimd.memset(ident[:], 0.0))
            link(nc.gpsimd.affine_select(out=ident[:], in_=ident[:], compare_op=ALU.not_equal, fill=1.0, base=0,
                                         pattern=[[-1, P]], channel_multiplier=1))
            link(nc.gpsimd.memset(mean_w[:], 1.0 / DM))
            link(nc.gpsimd.memset(combT, 1.0))
            link(nc.gpsimd.memset(sel[:], 0.0))
            for k in range(PARTS):
                link(nc.gpsimd.affine_select(out=sel[:], in_=sel[:], compare_op=ALU.not_equal, fill=1.0, base=-k * NX,
                                             pattern=[[-1, NX]], channel_multiplier=1))
            for k, value in enumerate((EPS, -0.5, -1.0)):
                link(nc.gpsimd.memset(consts[:, k:k + 1], value))
            for k in range(NX):
                link(nc.gpsimd.memset(expert_no[:, k:k + 1], float(k)))
            assert made[0] == POOL_CONSTS

            def softplus_sum(w, par):
                pool.wait_ge(softplus, 3 * w + 3)
                pool.wait_ge(sp_fix, 2 * w + 2)
                nc.gpsimd.tensor_tensor(sp_l[:], sp_l[:], sp_w[:], ALU.add).then_inc(sp_sum, 1)
                pool.wait_ge(sp_sum, w + 1)
                nc.gpsimd.tensor_tensor(delta[:, par, :], delta[:, par, :], sp_l[:], ALU.add).then_inc(delta_ready, 1)

            def z_affine(w):
                pool.wait_ge(z_stats, 2 * w + 2)
                wait(pool, siluz_ready, w)
                nc.gpsimd.tensor_tensor(z_ln[:, 0:1], z_mv[:, 1:2], eps, ALU.add)
                nc.gpsimd.tensor_tensor(z_ln[:, 1:2], z_mv[:, 0:1], minus_one, ALU.mult).then_inc(z_scale, 1)
                pool.wait_ge(z_scale, 3 * w + 1)
                nc.gpsimd.tensor_tensor(z_ln[:, 2:3], z_ln[:, 0:1], minus_half, ALU.pow).then_inc(z_scale, 1)
                pool.wait_ge(z_scale, 3 * w + 2)
                nc.gpsimd.tensor_tensor(z_ln[:, 3:4], z_ln[:, 1:2], z_ln[:, 2:3], ALU.mult).then_inc(z_scale, 1)

            def residual(w, c):
                pool.wait_ge(gated, w + 1)
                pool.wait_ge(res_loaded, DMA * (w + 1))
                nc.gpsimd.tensor_tensor(x2[:, c, :], x2[:, c, :], x_res[:], ALU.add).then_inc(x2_ready, 1)

            def body(b):
                for c in range(NW):
                    w = NW * b + c
                    for g in range(NG):
                        if b_scan(b):
                            i = GB * b + NG * c + g
                            slot = (NG * c + g) % RING
                            if g == 1:
                                z_affine(w)
                        if g == 2 and (b_scan(b) and not is_int(b, 0) or is_int(b, 0) and c > 0 or is_int(b, NB) and c == 0):
                            residual(w - 1, (c - 1) % NW)
                        if b_scan(b):
                            pool.wait_ge(scanned, i + 1)
                            if c == 0:
                                pool.wait_ge(c_loaded[g], DMA * (b + 1))
                            nc.gpsimd.tensor_tensor(ring[:, slot], ring[:, slot], bc[:, g, 1], ALU.mult).then_inc(weighted, 1)
                        if ("dt", c) in outs_of_slot(b, c, g, 2):
                            softplus_sum(w + 1, (c + 1) % 2)

            each_batch(pool, body)

        @block.scalar
        def _(act):
            act.wait_ge(ssm_loaded, DMA * N_SSM)
            nc.scalar.activation(a_neg[:], a_neg[:], ACT.Exp).then_inc(act_consts, 1)
            nc.scalar.activation(gates[:, 0:1], gates[:, 0:1], ACT.Tanh).then_inc(act_consts, 1)
            act.wait_ge(pool_consts, POOL_CONSTS)
            act.wait_ge(dve_consts, 2)

            def exps(b, c, g):
                w, i = NW * b + c, GB * b + NG * c + g
                if g == 0:
                    act.wait_ge(delta_ready, w + 1)
                wait(act, scanned, i - 1)
                for n in range(PAIR):
                    last = nc.scalar.activation(decay[:, g % 2, n, 1:L], delta[:, c % 2, 1:L], ACT.Exp,
                                                scale=a_neg[:, c, PAIR * g + n:PAIR * g + n + 1])
                last.then_inc(exp_ready, 1)

            def in_proj_out(b, c):
                bank = wait_filled(act, b, "in_proj", c)
                wait(act, conv_step, (TAPS - 1) * (NW * (b + 1) + c))
                nc.scalar.activation(xpad[:, TAPS - 1:], wk[:, bank, :], ACT.Copy)
                if not is_int(b, -1):
                    if c == NW - 1:
                        act.wait_ge(u_copied, DMA * (b + 1))
                    else:
                        act.wait_ge(skipped, NW * b + c + 1)
                nc.scalar.activation(u[:, c, :], wk[:, bank, :], ACT.Identity, scale=conv_taps[:, c, TAPS - 1:TAPS],
                                     bias=conv_bias[:, c:c + 1]).then_inc(drained[bank], 1)

            def silu_u(b, c):
                act.wait_ge(conv_step, (TAPS - 1) * (NW * (b + 1) + c + 1))
                nc.scalar.activation(u[:, c, :], u[:, c, :], ACT.Silu).then_inc(u_ready, 1)

            def silu_z(b, c):
                w = NW * b + c
                act.wait_ge(z_scale, 3 * w + 3)
                nc.scalar.activation(z[:, c % 2, :], z[:, c % 2, :], ACT.Silu, scale=z_ln[:, 2:3],
                                     bias=z_ln[:, 3:4]).then_inc(siluz_ready, 1)

            def dt_softplus(b, c):
                w, cn = NW * b + c + 1, (c + 1) % NW
                bank = wait_filled(act, b, "dt", c)
                wait(act, sp_fix, 2 * w)
                wait(act, softplus, 3 * w)
                nc.scalar.activation(sp_e[:], wk[:, bank, :], ACT.Abs, bias=dt_bias[:, cn:cn + 1]).then_inc(softplus, 1)
                wait(act, du_ready, w - 1)
                wait(act, exp_ready, NG * (w - 1))
                nc.scalar.activation(delta[:, cn % 2, :], wk[:, bank, :], ACT.Relu, bias=dt_bias[:, cn:cn + 1]).then_inc(drained[bank], 1)
                act.wait_ge(softplus, 3 * w + 1)
                nc.scalar.activation(sp_e[:], sp_e[:], ACT.Exp, scale=-1.0).then_inc(softplus, 1)
                act.wait_ge(softplus, 3 * w + 2)
                wait(act, delta_ready, w)
                nc.scalar.activation(sp_l[:], sp_e[:], ACT.Ln, bias=1.0).then_inc(softplus, 1)

            def jobs_out(b, c, g):
                m = b - 1
                for name, k in outs_of_slot(b, c, g):
                    if name == "in_proj":
                        in_proj_out(b, k)
                    if name == "x_proj":
                        bank = wait_filled(act, b, name)
                        wait(act, xdbl_stored, DMA * (b + 1))
                        nc.scalar.activation(x_dbl, wk[0:R + 2 * NS, bank, :], ACT.Copy).then_inc(drained[bank], 1)
                    if name == "dt":
                        dt_softplus(b, k)
                    if name == "var":
                        bank = wait_filled(act, b, name)
                        nc.scalar.activation(wk[:, bank, :], wk[:, bank, :], ACT.Ln, bias=eps).then_inc(rstd_step, 1)
                        act.wait_ge(rstd_step, 2 * m + 1)
                        nc.scalar.activation(wk[:, bank, :], wk[:, bank, :], ACT.Exp, scale=-0.5).then_inc(rstd_step, 1)
                    if name == "logits":
                        act.wait_ge(route_step, ROUTE_STEPS * m + 4)
                        nc.scalar.activation(share[:, 1], share[:, 0], ACT.Exp).then_inc(route_exp, 1)
                    if name == "comb":
                        bank = wait_filled(act, b, name)
                        nc.scalar.activation(combT[0:NC, :], wk[0:NC, bank, :], ACT.Copy)
                        nc.scalar.activation(comb_parts[:], wk[0:NC, bank, :], ACT.Copy).then_inc(drained[bank], 1)
                    if name == "down":
                        bank = wait_filled(act, b, name, k)
                        nc.scalar.activation(h[:, k, :], wk[:, bank, :], ACT.Identity, bias=b_down[:, k:k + 1]).then_inc(drained[bank], 1)
                if b_ffn(b) and (c, g) == SQUARE_SLOT:
                    wait_drained(act, b, "mean")
                    wait(act, out_stored[(NW - 1) % 2], DMA * 2 * m)
                    nc.scalar.activation(h[:, 0:NW, :], xn[:], ACT.Square).then_inc(squared, 1)

            def gelus(b, c, g):
                for slot, first, end in GELUS:
                    if b_ffn(b) and slot == (c, g):
                        for j in range(end - 2, end):
                            wait_drained(act, b, "down", j)
                        nc.scalar.activation(h[:, first:end, :], h[:, first:end, :], ACT.Gelu).then_inc(gelu_done, 1)

            def body(b):
                if is_int(b, 0):
                    act.wait_ge(ffn_loaded, DMA * N_FFN)
                    nc.scalar.activation(gates[:, 1:2], gates[:, 1:2], ACT.Tanh).then_inc(act_consts, 1)
                for c in range(NW):
                    for g in range(NG):
                        if b_scan(b):
                            if g < NG - 1:
                                exps(b, c, g + 1)
                            elif c < NW - 1:
                                exps(b, c + 1, 0)
                            elif not is_int(b, NB - 1):
                                exps(b + 1, 0, 0)
                        jobs_out(b, c, g)
                        if b_scan(b) and g == 4:
                            silu_z(b, c)
                        if b_prep(b) and (c, g) in SILUS:
                            silu_u(b, SILUS[c, g])
                        gelus(b, c, g)
                if is_int(b, -1):
                    exps(0, 0, 0)

            each_batch(act, body)

        @block.vector
        def _(dve):
            nc.vector.memset(xpad[:, 0:TAPS - 1], 0.0)
            nc.vector.memset(decay[:, :, :, 0:1], 0.0).then_inc(dve_consts, 1)
            dve.wait_ge(act_consts, 1)
            nc.vector.tensor_scalar(a_neg[:], a_neg[:], -1.0, None, ALU.mult).then_inc(dve_consts, 1)
            def delta_u(b, c):
                w = NW * b + c
                dve.wait_ge(delta_ready, w + 1)
                u_there(dve, b, c)
                wait(dve, outer_ready, NG * w)
                nc.vector.tensor_tensor(du[:], delta[:, c % 2, :], u[:, u_place(c), :], ALU.mult).then_inc(du_ready, 1)
                dve.wait_ge(du_ready, w + 1)

            def group(b, c, g):
                i = GB * b + NG * c + g
                slot = (NG * c + g) % RING
                if c == 0:
                    dve.wait_ge(b_loaded[g], DMA * (b + 1))
                if g % 2 == 0:
                    wait(dve, summed, (GB // 2) * b + (NG * c + g - RING) // 2 + 1)
                else:
                    wait(dve, paired, (GB // 2) * b + (NG * c + g - 1 - RING) // 2 + 1)
                nc.vector.tensor_tensor(ring[:, slot], du[:, None, :].broadcast_to([P, PAIR, L]), bc[:, g, 0],
                                        ALU.mult).then_inc(outer_ready, 1)
                dve.wait_ge(outer_ready, i + 1)
                dve.wait_ge(exp_ready, i + 1)
                states = ring[:, slot].rearrange("p n l -> p (n l)")
                nc.vector.tensor_tensor_scan(states, decay[:, g % 2].rearrange("p n l -> p (n l)"), states, 0.0,
                                             ALU.mult, ALU.add).then_inc(scanned, 1)

            def skip(b, c):
                w, slot = NW * b + c, NG * c % RING
                dve.wait_ge(weighted, NG * w + 1)
                nc.vector.scalar_tensor_tensor(ring[:, slot, 0, :], u[:, u_place(c), :], d_skip[:, c:c + 1],
                                               ring[:, slot, 0, :], ALU.mult, ALU.add).then_inc(skipped, 1)

            def add_pair(b, k):
                slot = k % RING
                dve.wait_ge(weighted, GB * b + k + 2)
                if k % NG == 0:
                    dve.wait_ge(skipped, NW * b + k // NG + 1)
                nc.vector.tensor_tensor(ring[:, slot], ring[:, slot], ring[:, slot + 1], ALU.add).then_inc(paired, 1)

            def conv(b, c):
                wait_drained(dve, b, "in_proj", c)
                for k in range(TAPS - 1):
                    nc.vector.scalar_tensor_tensor(u[:, c, :], xpad[:, k:k + L], conv_taps[:, c, k:k + 1], u[:, c, :],
                                                   ALU.mult, ALU.add).then_inc(conv_step, 1)
                    if k < TAPS - 2:
                        dve.wait_ge(conv_step, (TAPS - 1) * (NW * (b + 1) + c) + k + 1)

            def stats_z(b, c):
                w = NW * b + c
                dve.wait_ge(z_loaded[c % 2], DMA * (2 * b + c // 2 + 1))
                wait(dve, z_scale, 3 * w)
                nc.vector.bn_stats(z_stat[:], z[:, c % 2, :]).then_inc(z_stats, 1)
                dve.wait_ge(z_stats, 2 * w + 1)
                apart(dve)
                nc.vector.bn_aggr(z_mv[:], z_stat[:]).then_inc(z_stats, 1)

            def gate(b, c):
                w = NW * b + c
                dve.wait_ge(summed, NG // 2 * (w + 1))
                dve.wait_ge(siluz_ready, w + 1)
                if not is_int(b, 0):
                    dve.wait_ge(x2_stored, DMA * b)
                nc.vector.scalar_tensor_tensor(x2[:, c, :], y[:], gates[:, 0:1], z[:, c % 2, :], ALU.mult,
                                               ALU.mult).then_inc(gated, 1)

            def softplus_fix(b, c):
                w = NW * b + c + 1
                dve.wait_ge(softplus, 3 * w + 2)
                wait(dve, delta_ready, w)
                nc.vector.tensor_scalar(sp_w[:], sp_e[:], 1.0, -1.0, ALU.add, ALU.add).then_inc(sp_fix, 1)
                dve.wait_ge(sp_fix, 2 * w + 1)
                nc.vector.scalar_tensor_tensor(sp_w[:], sp_w[:], -1.0, sp_e[:], ALU.mult, ALU.add).then_inc(sp_fix, 1)

            def centre(b):
                bank = wait_filled(dve, b, "mean")
                nc.vector.tensor_tensor(xn[:], x2[:], wk[:, bank, None, :].broadcast_to([P, NW, L]),
                                        ALU.subtract).then_inc(drained[bank], 1)
                wait_drained(dve, b, "mean")

            def normalise(b):
                m = b - 1
                bank, _ = work(b, "var")
                dve.wait_ge(rstd_step, 2 * m + 2)
                dve.wait_ge(squared, m + 1)
                nc.vector.tensor_tensor(xn[:], xn[:], wk[:, bank, None, :].broadcast_to([P, NW, L]),
                                        ALU.mult).then_inc(drained[bank], 1)

            def route(b):
                m = b - 1
                steps = [0]

                def link(ins):
                    steps[0] += 1
                    ins.then_inc(route_step, 1)
                    dve.wait_ge(route_step, ROUTE_STEPS * m + steps[0])

                def over_experts(t):
                    return t.broadcast_to([P, NT, NX])

                bank = wait_filled(dve, b, "logits")
                nc.vector.tensor_copy(logit[:].rearrange("p t x -> p (t x)"), wk[:, bank, 0:NT * NX]).then_inc(drained[bank], 1)
                wait_drained(dve, b, "logits")
                apart(dve)
                for t in range(NT):
                    last = nc.vector.max(top[:, t, :], logit[:, t, :])
                link(last)
                apart(dve)
                for t in range(NT):
                    last = nc.vector.max_index(top_no[:, t, :], top[:, t, :], logit[:, t, :])
                link(last)
                link(nc.vector.tensor_copy(top_f[:], top_no[:, :, 0:2]))
                link(nc.vector.tensor_tensor(share[:, 0], top[:, :, 1:2], top[:, :, 0:1], ALU.subtract))
                numbers = expert_no[:, None, :].broadcast_to([P, NT, NX])
                link(nc.vector.tensor_tensor(pick[:, 0], numbers, over_experts(top_f[:, :, 0:1]), ALU.is_equal))
                link(nc.vector.tensor_tensor(pick[:, 1], numbers, over_experts(top_f[:, :, 1:2]), ALU.is_equal))
                dve.wait_ge(route_exp, m + 1)
                link(nc.vector.tensor_scalar(share[:, 2], share[:, 1], 1.0, None, ALU.add))
                link(nc.vector.reciprocal(share[:, 2], share[:, 2]))
                link(nc.vector.tensor_tensor(share[:, 3], share[:, 1], share[:, 2], ALU.mult))
                link(nc.vector.tensor_tensor(pick[:, 0], pick[:, 0], over_experts(share[:, 2]), ALU.mult))
                link(nc.vector.tensor_tensor(pick[:, 1], pick[:, 1], over_experts(share[:, 3]), ALU.mult))
                link(nc.vector.tensor_tensor(pick[:, 2], pick[:, 0], pick[:, 1], ALU.add))
                link(nc.vector.tensor_copy(part16[:], pick[:, 2]))
                link(nc.vector.tensor_copy(parts[:, :, 0, :], part16[:]))
                link(nc.vector.tensor_tensor(pick[:, 2], pick[:, 2], parts[:, :, 0, :], ALU.subtract))
                link(nc.vector.tensor_copy(part16[:], pick[:, 2]))
                link(nc.vector.tensor_copy(parts[:, :, 1, :], part16[:]))
                link(nc.vector.tensor_tensor(parts[:, :, 2, :], pick[:, 2], parts[:, :, 1, :], ALU.subtract))
                link(nc.vector.tensor_copy(top_f[:, :, 0:1], share[:, 0]))
                assert steps[0] == ROUTE_STEPS

            def mix(b, k):
                m = b - 1
                bank = wait_filled(dve, b, "mix", k)
                dve.wait_ge(gelu_done, len(GELUS) * m + (1 if k < GELUS[0][2] else 2))
                nc.vector.tensor_tensor(h[:, k, :], h[:, k, :], wk[:, bank, :], ALU.mult).then_inc(drained[bank], 1)

            def up_out(b, d):
                m = b - 1
                bank = wait_filled(dve, b, "up", d)
                dve.wait_ge(x2_loaded[d % 2], DMA * (2 * m + d // 2 + 1))
                nc.vector.scalar_tensor_tensor(x_out[:, d % 2, :], wk[:, bank, :], gates[:, 1:2], x_out[:, d % 2, :],
                                               ALU.mult, ALU.add).then_inc(drained[bank], 1)

            def body(b):
                for c in range(NW):
                    for g in range(NG):
                        if g == 2 and (b_scan(b) and not is_int(b, 0) or is_int(b, 0) and c > 0 or is_int(b, NB) and c == 0):
                            if c == 0:
                                gate(b - 1, NW - 1)
                            else:
                                gate(b, c - 1)
                        if b_scan(b):
                            if g == 0:
                                delta_u(b, c)
                            group(b, c, g)
                            if g == 0:
                                stats_z(b, c)
                            if g == 1:
                                skip(b, c)
                        if g % 2 == 0:
                            k = NG * c + g - LAG
                            if k >= 0 and b_scan(b):
                                add_pair(b, k)
                            elif k < 0 and b_ffn(b):
                                add_pair(b - 1, GB + k)
                        if b_prep(b) and (c, g) in CONVS:
                            conv(b, CONVS[c, g])
                        if ("dt", c) in outs_of_slot(b, c, g, 2):
                            softplus_fix(b, c)
                        for name, k in outs_of_slot(b, c, g):
                            if name == "mean":
                                centre(b)
                            if name == "var":
                                normalise(b)
                            if name == "logits":
                                route(b)
                            if name == "mix":
                                mix(b, k)
                            if name == "up":
                                up_out(b, k)
                if is_int(b, 0):
                    dve.wait_ge(act_consts, 3)

            dve.wait_ge(act_consts, 2)
            each_batch(dve, body)

        @block.tensor
        def _(pe):
            pe.wait_ge(ssm_loaded, DMA * N_SSM)
            pe.wait_ge(pool_consts, POOL_CONSTS)

            def sum_pair(b, k):
                slot, first, last = k % RING, k % NG == 0, k % NG == NG - 2
                if first:
                    wait(pe, gated, NW * b + k // NG)
                pe.wait_ge(paired, (GB // 2) * b + k // 2 + 1)
                for n in range(PAIR):
                    add = nc.tensor.matmul(y[:], ident[:], ring[:, slot, n, :], start=first and n == 0,
                                           stop=last and n == PAIR - 1)
                add.then_inc(summed, 1)

            def job(b, name, k):
                m = b - 1
                bank, n = work(b, name, k)
                wait(pe, drained[bank], n - 1)
                o = wk[:, bank, :]
                if name == "in_proj":
                    if k == 0:
                        pe.wait_ge(ctx_loaded, DMA * (b + 2))
                    for j in range(KC):
                        last = nc.tensor.matmul(o, in_w[:, j, k * P:(k + 1) * P], ctx_in[:, j, :], start=j == 0, stop=j == KC - 1)
                if name == "x_proj":
                    pe.wait_ge(u_ready, NW * (b + 2))
                    for j in range(NW):
                        last = nc.tensor.matmul(o[0:R + 2 * NS, :], xp_w[:, j, :], u[:, j, :], start=j == 0, stop=j == NW - 1)
                if name == "dt":
                    if k == NW - 1:
                        wait_drained(pe, b, "x_proj")
                    kn = (k + 1) % NW
                    last = nc.tensor.matmul(o, dt_w[:, kn * P:(kn + 1) * P], x_dbl[0:R, :], start=True, stop=True)
                if name == "mean":
                    pe.wait_ge(x2_ready, NW * b)
                    for j in range(NW):
                        last = nc.tensor.matmul(o, mean_w[:], x2[:, j, :], start=j == 0, stop=j == NW - 1)
                if name == "var":
                    pe.wait_ge(squared, m + 1)
                    for j in range(NW):
                        last = nc.tensor.matmul(o, mean_w[:], h[:, j, :], start=j == 0, stop=j == NW - 1)
                if name == "logits":
                    wait_drained(pe, b, "var")
                    for t in range(NT):
                        for j in range(NW):
                            last = nc.tensor.matmul(o[:, t * NX:(t + 1) * NX], xn[:, j, t * P:(t + 1) * P], gate_w[:, j, :],
                                                    start=j == 0, stop=j == NW - 1)
                if name == "comb":
                    pe.wait_ge(route_step, ROUTE_STEPS * b)
                    for t in range(NT):
                        last = nc.tensor.transpose(o[0:NC, t * P:(t + 1) * P],
                                                   parts[:, t].rearrange("p i x -> p (i x)"), ident[:])
                if name == "down":
                    for j in range(NW):
                        last = nc.tensor.matmul(o, w_down[:, j, k, :], xn[:, j, :], start=j == 0, stop=j == NW - 1)
                if name == "mix":
                    if k == 0:
                        wait_drained(pe, b, "comb")
                    last = nc.tensor.matmul(o, sel[:, k:k + 1].broadcast_to([NC, P]), comb_parts[:], start=True, stop=True)
                if name == "up":
                    if k == 0:
                        wait_mixed(b, bank, UP_SPLIT, NX)
                        pe.wait_ge(gelu_done, len(GELUS) * b)
                    for j in range(UP_SPLIT, NE):
                        last = nc.tensor.matmul(o, w_up[:, j, k * P:(k + 1) * P], h[:, j, :], start=False, stop=j == NE - 1)
                last.then_inc(filled[bank], 1)

            def wait_mixed(b, bank, first, end):
                last = [k for k in range(first, end) if work(b, "mix", k)[0] != bank]
                if last:
                    wait_drained(pe, b, "mix", last[-1])

            def start_up(b, k):
                bank, n = work(b, "up", k)
                wait(pe, drained[bank], n - 1)
                if k == 0:
                    wait_mixed(b, bank, 0, UP_SPLIT)
                nc.tensor.matmul(wk[:, bank, :], b_up[:, k * P:(k + 1) * P], combT, start=True, stop=False)
                for j in range(UP_SPLIT):
                    nc.tensor.matmul(wk[:, bank, :], w_up[:, j, k * P:(k + 1) * P], h[:, j, :], start=False, stop=False)

            def body(b):
                for c in range(NW):
                    for g in range(NG):
                        for name, j in jobs_of_slot(b, c, g):
                            job(b, name, j)
                        if b_ffn(b) and (c, g) in UP_STARTS:
                            start_up(b, UP_STARTS[c, g])
                        k = NG * c + g - LAG
                        if k % 2 == 0 and k >= 0 and b_scan(b):
                            sum_pair(b, k)
                        elif k % 2 == 0 and k < 0 and b_ffn(b):
                            sum_pair(b - 1, GB + k)
                if is_int(b, 0):
                    pe.wait_ge(ffn_loaded, DMA * N_FFN)

            each_batch(pe, body)


_INS = ['x', 'xT', 'ctxT', 'g_xattn', 'g_ffn', 'in_wT', 'conv_w', 'conv_b', 'xp_wT', 'dt_wT', 'dt_b', 'A_log', 'D',
        'gate_wT', 'wdT', 'bdT', 'wuT', 'bu', 'ws_dT', 'bs_d', 'ws_uT', 'bs_u']


def kernel(x, ctx_1024, g_xattn, g_ffn, L0_xattn_in_proj_w, L0_xattn_conv_w, L0_xattn_conv_b, L0_xattn_x_proj_w,
           L0_xattn_dt_proj_w, L0_xattn_dt_proj_b, L0_xattn_A_log, L0_xattn_D, L0_ffn_gate_w, L0_ffn_wd, L0_ffn_bd,
           L0_ffn_wu, L0_ffn_bu, L0_ffn_ws_d, L0_ffn_bs_d, L0_ffn_ws_u, L0_ffn_bs_u):
    import numpy as np
    import concourse.bacc as bacc
    from concourse.bass_utils import run_bass_kernel_spmd

    def by_partition(t):
        t = np.asarray(t)
        return np.swapaxes(t.reshape((NW, P) + t.shape[1:]), 0, 1)

    laid = {
        'x': x, 'xT': np.transpose(x, (0, 2, 1)), 'ctxT': np.transpose(ctx_1024, (0, 2, 1)),
        'g_xattn': g_xattn, 'g_ffn': g_ffn, 'in_wT': np.transpose(L0_xattn_in_proj_w),
        'conv_w': by_partition(L0_xattn_conv_w), 'conv_b': by_partition(L0_xattn_conv_b), 'xp_wT': np.transpose(L0_xattn_x_proj_w),
        'dt_wT': np.transpose(L0_xattn_dt_proj_w), 'dt_b': by_partition(L0_xattn_dt_proj_b), 'A_log': by_partition(L0_xattn_A_log),
        'D': by_partition(L0_xattn_D), 'gate_wT': np.transpose(L0_ffn_gate_w), 'wdT': np.transpose(L0_ffn_wd, (2, 0, 1)),
        'bdT': np.transpose(L0_ffn_bd), 'wuT': np.transpose(L0_ffn_wu, (2, 0, 1)), 'bu': L0_ffn_bu,
        'ws_dT': np.transpose(L0_ffn_ws_d), 'bs_d': L0_ffn_bs_d, 'ws_uT': np.transpose(L0_ffn_ws_u),
        'bs_u': L0_ffn_bs_u,
    }
    nc = bacc.Bacc("TRN2", target_bir_lowering=False, num_devices=1)
    arrays, args = {}, []
    for name in _INS:
        a = np.ascontiguousarray(laid[name])
        arrays[f"in_{name}"] = a
        args.append(nc.dram_tensor(f"in_{name}", a.shape, mybir.dt.from_np(a.dtype), kind="ExternalInput").ap())
    out = nc.dram_tensor("out_T", (NB, DM, L), F32, kind="ExternalOutput").ap()
    mamba_moe_kernel(nc, *args, out)
    r = run_bass_kernel_spmd(nc, [arrays], core_ids=[0])
    return np.ascontiguousarray(np.transpose(r.results[0]["out_T"], (0, 2, 1)))
```

```python
from contextlib import ExitStack

import concourse.bass as bass
from concourse import mybir

ALU = mybir.AluOpType
ACT = mybir.ActivationFunctionType
F32 = mybir.dt.float32
BF16 = mybir.dt.bfloat16
U32 = mybir.dt.uint32

P = 128
NB = 4
L = 512
DM = 512
DCTX = 256
KC = DCTX // P
NW = DM // P
NS = 16
PAIR = 2
NG = NS // PAIR
GB = NW * NG
R = 16
TAPS = 4
PADDED = TAPS - 1 + L
NX = 8
NE = NX + 1
NT = L // P
RING = 4
LAG = 2
EPS = 1e-5
DMA = 16
PARTS = 3
SHARE_PART = [0, 0, 0, 1, 1, 2]
BIAS_PART = [0, 1, 2, 0, 1, 0]
NC = len(SHARE_PART) * NX
NR = NC + PARTS
BIAS_STEPS = 7
POOL_CONSTS = 8 + PARTS + NX
PICK_STEPS = 6
ROUTE_STEPS = 17


JOBS = {
    "y": [0, 9, 17, 25],
    "in_proj": [0, 10, 17, 21],
    "mean": [2],
    "x_proj": [25],
    "var": [7],
    "dt": [2, 10, 18, 26],
    "scale": [8],
    "up": [19, 22, 23, 26],
    "logits": [9],
    "comb": [11],
    "down": [5, 7, 8, 10, 11, 11, 14, 15, 16],
    "mix": [12, 14, 15, 16, 16, 17, 16, 18],
}
READS = {
    "y": [2, 11, 19, 27],
    "in_proj": [1.5, 11, 18.5, 22.5],
    "var": [6.5],
    "x_proj": [26.5],
    "mean": [5],
    "dt": [4.5, 12.5, 20.5, 28.5],
    "down": [7.5, 8.5, 10, 12.5, 13.5, 14, 16, 16.5, 17.5],
    "logits": [11.5],
    "scale": [9],
    "mix": [15, 16, 17, 17.5, 17.5, 18.5, 17.5, 20],
    "comb": [14],
    "up": [21.5, 24, 27.5, 31],
}
STEPS = {
    "start_up": [18, 21, 22, 25],
    "skip": [1.5, 9.5, 17.5, 25.5],
    "conv": [3.5, 11.5, 20.5, 22.5],
    "fix": [5.5, 13.5, 21.5, 29.5],
    "shares": [11.5],
    "add": [5, 7, 13, 15, 21, 22, 29, 31],
    "share_exp": [11.5],
    "square": [6],
    "silu_z": [4.5, 13, 21, 29.5],
    "silu_u": [5, 12.5, 20.5, 23.5],
    "gelu": [13.5, 17.5, 19],
}
PROLOGUE = {
    ("job", "in_proj"): [0, 1, 2, 3], ("job", "x_proj"): [6],
    ("step", "in_proj"): [1.5, 2.5, 3.5, 4.5], ("step", "x_proj"): [7],
    ("step", "conv"): [2.5, 3.5, 4.5, 5.5], ("step", "silu_u"): [3, 4, 5, 6],
}
UP_SPLIT = 4
GELUS = [(0, UP_SPLIT), (UP_SPLIT, 7), (7, NE)]
PAIRS = NG // 2


def windows_before(b, c):
    return is_int(b, 0) and c > 0 or b_ffn(b) and (b_scan(b) or c == 0)


def takes_part(b, name, k):
    if name == "y":
        return windows_before(b, k)
    if name in ("dt", "fix"):
        return (b_scan(b) or k == NW - 1) and not is_int(b, NB) and not (is_int(b, NB - 1) and k == NW - 1)
    if name in ("skip", "silu_z", "add"):
        return b_scan(b)
    if name in ("in_proj", "x_proj", "conv", "silu_u"):
        return b_prep(b)
    return b_ffn(b)


def due(b, time, *tables):
    if is_int(b, -1):
        tables = [{name: PROLOGUE.get((kind, name), table[name]) for name in table}
                  for kind, table in (("job" if table is JOBS else "step", table) for table in tables)]
    return [(name, k) for table in tables for name in table for k, t in enumerate(table[name])
            if t == time and takes_part(b, name, k)]


def is_int(b, value):
    return isinstance(b, int) and b == value


def b_prep(b):
    return not (isinstance(b, int) and b >= NB - 1)


def b_ffn(b):
    return not (isinstance(b, int) and b <= 0)


def b_scan(b):
    return not (isinstance(b, int) and (b < 0 or b == NB))


def jobs_of_body(b):
    return [job for slot in range(GB) for job in due(b, slot, JOBS)]


BEFORE_FIRST = len(jobs_of_body(-1))
BEFORE_FULL = BEFORE_FIRST + len(jobs_of_body(0))
PER_FULL = len(jobs_of_body(1))
WORK_BANKS = 3
assert PER_FULL % WORK_BANKS == 0, PER_FULL
ORDER = {b: jobs_of_body(b) for b in range(-1, NB + 1)}
BEFORE = {-1: 0, 0: BEFORE_FIRST, NB: BEFORE_FULL + (NB - 2) * PER_FULL + len(ORDER[NB - 1])}
BEFORE.update({b: BEFORE_FULL + (b - 1) * PER_FULL for b in range(1, NB)})


def work(b, name, k=0):
    if isinstance(b, int):
        j = BEFORE[b] + ORDER[b].index((name, k))
        return j % WORK_BANKS, j // WORK_BANKS + 1
    j = BEFORE_FULL - PER_FULL + ORDER[1].index((name, k))
    return j % WORK_BANKS, b * (PER_FULL // WORK_BANKS) + (j // WORK_BANKS + 1)


def mamba_moe_kernel(nc, x, xT, ctxT, g_xattn, g_ffn, in_wT, conv_w, conv_b, xp_wT, dt_wT, dt_b, A_log, D,
                     gate_wT, wdT, bdT, wuT, bu, ws_dT, bs_d, ws_uT, bs_u, mask, out):
    bc_dram = nc.dram_tensor("bc_scratch", (NB, 2 * NS, L), F32, kind="Internal").ap()
    x2_dram = nc.dram_tensor("x2_scratch", (NB, DM, L), F32, kind="Internal").ap()

    with ExitStack() as ctx:
        def sb(name, shape, dt=F32):
            return ctx.enter_context(nc.sbuf_tensor(name, shape, dt))

        def sem(name):
            return ctx.enter_context(nc.semaphore(name))

        decay = ctx.enter_context(nc.psum_tensor("decay", [P, 2, PAIR, L], F32))
        du = ctx.enter_context(nc.psum_tensor("du", [P, L], F32))
        wk = ctx.enter_context(nc.psum_tensor("wk", [P, WORK_BANKS, L], F32))

        in_w = sb("in_w", [P, KC, DM])
        xp_w = sb("xp_w", [P, NW, R + 2 * NS])
        dt_w = sb("dt_w", [R, DM])
        b_up = sb("b_up", [NR, DM], BF16)
        part_mask = sb("part_mask", [NR, PARTS])
        gate_w = sb("gate_w", [P, NW, NX])
        w_down = sb("w_down", [P, NW, NE, P])
        w_up = sb("w_up", [P, NE, DM])
        conv_taps = sb("conv_taps", [P, NW, TAPS])
        conv_bias = sb("conv_bias", [P, NW])
        dt_bias = sb("dt_bias", [P, NW])
        d_skip = sb("d_skip", [P, NW])
        b_down = sb("b_down", [P, NE])
        a_neg = sb("a_neg", [P, NW, NS])
        ident = sb("ident", [P, P])
        sel = sb("sel", [NR, NX], BF16)
        expert_no = sb("expert_no", [P, NX])
        consts = sb("consts", [P, 6])
        gates = consts[:, 4:6]
        eps, minus_half, minus_one, one_of_dm = (consts[:, k:k + 1] for k in range(4))
        mean_w = one_of_dm.broadcast_to([P, P])

        ctx_in = sb("ctx_in", [P, KC, L])
        xpad = sb("xpad", [P, TAPS - 1 + L])
        sp_w = xpad[:, TAPS - 1:]
        u = sb("u", [P, NW + 1, L])
        x_dbl = sb("x_dbl", [R + 2 * NS, L])
        comb_parts = sb("comb_parts", [NR, L], BF16)
        sp_e = sb("sp_e", [P, L])
        sp_l = sb("sp_l", [P, L])
        delta = sb("delta", [P, 2, L])
        bc = sb("bc", [P, NG, 2, PAIR, L])
        z = sb("z", [P, 2, L])
        z_stat = sb("z_stat", [P, 6])
        z_small = sb("z_small", [P, 6])
        z_mv, z_ln = z_small[:, 0:2], z_small[:, 2:6]

        ring = sb("ring", [P, RING, PAIR, L])
        pair_sum = sb("pair_sum", [P, 2, PAIR, L])
        x_res = sb("x_res", [P, L])
        x2 = sb("x2", [P, NW, L])

        xc = sb("xc", [P, NW, L])
        rstd = sb("rstd", [P, L])
        x_sum = rstd[:]
        h = sb("h", [P, NE, L])
        squares = h[:, NE - NW:NE, :]
        bias_rows, bias_rest, bias_sum = (h[0:NR, k, :] for k in range(NE - 3, NE))
        logit = sb("logit", [P, NT, NX])
        rstd_col = sb("rstd_col", [P, NT, 1])
        top = sb("top", [P, NT, NX])
        top_no = sb("top_no", [P, NT, NX], U32)
        top_f = sb("top_f", [P, NT, 2])
        share = sb("share", [P, 4, NT, 1])
        pick = sb("pick", [P, 3, NT, NX])
        part16 = sb("part16", [P, 2, NT, NX], BF16)
        parts = sb("parts", [P, NT, len(SHARE_PART), NX])
        x_out = sb("x_out", [P, 2, L])

        in_w_loaded = sem("in_w_loaded")
        ssm_loaded = sem("ssm_loaded")
        ffn_loaded = sem("ffn_loaded")
        bias_loaded = sem("bias_loaded")
        bias_step = sem("bias_step")
        pool_consts = sem("pool_consts")
        dve_consts = sem("dve_consts")
        act_consts = sem("act_consts")
        ctx_loaded = sem("ctx_loaded")
        z_loaded = [sem(f"z_loaded{k}") for k in range(2)]
        res_loaded = sem("res_loaded")
        u_copied = sem("u_copied")
        xdbl_stored = sem("xdbl_stored")
        b_loaded = [sem(f"b_loaded{k}") for k in range(NG)]
        c_loaded = [sem(f"c_loaded{k}") for k in range(NG)]
        x2_stored = sem("x2_stored")
        x2_loaded = [sem(f"x2_loaded{k}") for k in range(2)]
        out_stored = [sem(f"out_stored{k}") for k in range(2)]
        filled = [sem(f"filled{k}") for k in range(WORK_BANKS)]
        drained = [sem(f"drained{k}") for k in range(WORK_BANKS)]
        u_ready = sem("u_ready")
        softplus = sem("softplus")
        sp_fix = sem("sp_fix")
        sp_sum = sem("sp_sum")
        delta_ready = sem("delta_ready")
        du_ready = sem("du_ready")
        exp_ready = sem("exp_ready")
        outer_ready = sem("outer_ready")
        scanned = sem("scanned")
        weighted = sem("weighted")
        skipped = sem("skipped")
        paired = sem("paired")
        pair_added = sem("pair_added")
        conv_step = sem("conv_step")
        z_stats = sem("z_stats")
        z_scale = sem("z_scale")
        siluz_ready = sem("siluz_ready")
        gated = sem("gated")
        x2_ready = sem("x2_ready")
        x_summed = sem("x_summed")
        squared = sem("squared")
        rstd_ready = sem("rstd_ready")
        route_step = sem("route_step")
        route_exp = sem("route_exp")
        gelu_done = sem("gelu_done")

        passed = sem("passed")

        block = ctx.enter_context(nc.Block())
        N_SSM = 8
        N_FFN = 8
        N_BIAS = len(BIAS_PART) + PARTS + 1

        def wait(eng, s, value):
            if not isinstance(value, int) or value > 0:
                eng.wait_ge(s, value)

        def wait_filled(eng, b, name, k=0):
            bank, n = work(b, name, k)
            eng.wait_ge(filled[bank], n)
            return bank

        def wait_drained(eng, b, name, k=0):
            bank, n = work(b, name, k)
            eng.wait_ge(drained[bank], n)

        def apart(eng):
            eng.sem_inc(passed, 1)

        def padded(b, c):
            if not is_int(b, -1):
                return xpad[:]
            return h[:].rearrange("p k l -> p (k l)")[:, c * PADDED:(c + 1) * PADDED]

        def u_place(c):
            return NW if c == NW - 1 else c

        def u_there(eng, b, c):
            if c == NW - 1:
                eng.wait_ge(u_copied, DMA * (b + 1))
            else:
                eng.wait_ge(u_ready, NW * b + c + 1)

        def each_batch(eng, body):
            body(-1)
            body(0)
            with eng.Fori(1, NB - 1) as b:
                body(b)
            body(NB - 1)
            body(NB)

        @block.sync
        def _(sp):
            def load_z(bb, c):
                wait(sp, gated, NW * bb + c - 1)
                apart(sp)
                sp.dma_start(z[:, c % 2, :], x[bb, c * P:(c + 1) * P, :]).then_inc(z_loaded[c % 2], DMA)

            def load_bc(m, g):
                wait(sp, outer_ready, GB * (m - 1) + GB - NG + g + 1)
                wait(sp, weighted, GB * (m - 1) + GB - NG + g + 1)
                apart(sp)
                for k, s in ((0, b_loaded[g]), (1, c_loaded[g])):
                    rows = bc_dram[m, k * NS + PAIR * g:k * NS + PAIR * g + PAIR, :].rearrange("n l -> (n l)")
                    sp.dma_start(bc[:, g, k].rearrange("p n l -> p (n l)"),
                                 rows.rearrange("(o f) -> o f", o=1).broadcast_to([P, PAIR * L])).then_inc(s, DMA)

            def reload_x2(m, d):
                wait(sp, x2_stored, DMA * (m + 1))
                wait(sp, out_stored[d % 2], DMA * (2 * m + d // 2 + 1))
                apart(sp)
                sp.dma_start(x_out[:, d % 2, :], x2_dram[m, d * P:(d + 1) * P, :]).then_inc(x2_loaded[d % 2], DMA)

            def store_out(b, m, d):
                wait_drained(sp, b, "up", d)
                apart(sp)
                sp.dma_start(out[m, d * P:(d + 1) * P, :], x_out[:, d % 2, :]).then_inc(out_stored[d % 2], DMA)

            for k in range(2):
                sp.sem_inc(out_stored[k], DMA)
            sp.dma_start(ctx_in[:], ctxT[0].rearrange("(k p) l -> p k l", p=P)).then_inc(ctx_loaded, DMA)
            sp.dma_start(in_w[:], in_wT.rearrange("(k p) e -> p k e", p=P)).then_inc(in_w_loaded, DMA)
            sp.dma_start(conv_taps[:], conv_w).then_inc(ssm_loaded, DMA)
            sp.dma_start(conv_bias[:], conv_b).then_inc(ssm_loaded, DMA)
            sp.dma_start(xp_w[:], xp_wT.rearrange("(c p) k -> p c k", p=P)).then_inc(ssm_loaded, DMA)
            sp.dma_start(dt_w[:], dt_wT).then_inc(ssm_loaded, DMA)
            sp.dma_start(dt_bias[:], dt_b).then_inc(ssm_loaded, DMA)
            sp.dma_start(a_neg[:], A_log).then_inc(ssm_loaded, DMA)
            sp.dma_start(d_skip[:], D).then_inc(ssm_loaded, DMA)
            sp.dma_start(gates[:, 0:1], g_xattn.rearrange("(o f) -> o f", o=1).broadcast_to([P, 1])).then_inc(ssm_loaded, DMA)
            load_z(0, 0)
            for k in range(len(BIAS_PART)):
                sp.dma_start(bias_rows[k * NX:(k + 1) * NX, :], bu).then_inc(bias_loaded, DMA)
            for k in range(PARTS):
                sp.dma_start(bias_rows[NC + k:NC + k + 1, :], bs_u.rearrange("(o d) -> o d", o=1)).then_inc(bias_loaded, DMA)
            sp.dma_start(part_mask[:], mask).then_inc(bias_loaded, DMA)
            sp.dma_start(gates[:, 1:2], g_ffn.rearrange("(o f) -> o f", o=1).broadcast_to([P, 1])).then_inc(ffn_loaded, DMA)
            sp.dma_start(gate_w[:], gate_wT.rearrange("(k p) x -> p k x", p=P)).then_inc(ffn_loaded, DMA)
            sp.dma_start(w_down[:, :, 0:NX, :], wdT.rearrange("(k p) x j -> p k x j", p=P)).then_inc(ffn_loaded, DMA)
            sp.dma_start(w_down[:, :, NX, :], ws_dT.rearrange("(k p) j -> p k j", p=P)).then_inc(ffn_loaded, DMA)
            sp.dma_start(w_up[:, 0:NX, :], wuT).then_inc(ffn_loaded, DMA)
            sp.dma_start(w_up[:, NX, :], ws_uT).then_inc(ffn_loaded, DMA)
            sp.dma_start(b_down[:, 0:NX], bdT).then_inc(ffn_loaded, DMA)
            sp.dma_start(b_down[:, NX:NE], bs_d.rearrange("(p o) -> p o", o=1)).then_inc(ffn_loaded, DMA)

            def copy_u(b):
                wait(sp, gated, NW * b)
                sp.wait_ge(u_ready, NW * (b + 1))
                apart(sp)
                sp.dma_start(u[:, NW, :], u[:, NW - 1, :]).then_inc(u_copied, DMA)

            def body(b):
                m = b - 1
                for c in range(NW):
                    if b_scan(b) and c == 1:
                        copy_u(b)
                    if b_ffn(b) and c == 3:
                        reload_x2(m, 2)
                        store_out(b, m, 1)
                        reload_x2(m, 3)
                    if b_scan(b):
                        if not (is_int(b, NB - 1) and c == NW - 1):
                            load_z(b + (c + 1) // NW, (c + 1) % NW) if c < NW - 1 else load_z(b + 1, 0)
                        wait(sp, x2_ready, NW * b + c)
                        apart(sp)
                        sp.dma_start(x_res[:], xT[b, c * P:(c + 1) * P, :]).then_inc(res_loaded, DMA)
                    if b_ffn(b) and c == 0:
                        wait(sp, x2_ready, NW * (m + 1))
                        apart(sp)
                        sp.dma_start(x2_dram[m].rearrange("(k p) l -> p k l", p=P), x2[:]).then_inc(x2_stored, DMA)
                    if b_ffn(b) and c == 1:
                        reload_x2(m, 0)
                        reload_x2(m, 1)
                    if b_ffn(b) and c == 2:
                        store_out(b, m, 0)
                    if b_prep(b) and c == 3:
                        wait_drained(sp, b, "x_proj")
                        apart(sp)
                        sp.dma_start(bc_dram[b + 1], x_dbl[R:R + 2 * NS, :]).then_inc(xdbl_stored, DMA)
                        sp.wait_ge(xdbl_stored, DMA * (b + 2))
                        for g in range(NG):
                            load_bc(b + 1, g)
                            if b_ffn(b) and g == 3:
                                store_out(b, m, 2)
                            if b_ffn(b) and g == 6:
                                store_out(b, m, 3)
                    elif b_ffn(b) and c == 3:
                        store_out(b, m, 2)
                        store_out(b, m, 3)
            each_batch(sp, body)
            for k in range(2):
                sp.wait_ge(out_stored[k], DMA * (2 * NB + 1))

        @block.gpsimd
        def _(pool):
            made = [0]

            def link(ins):
                made[0] += 1
                ins.then_inc(pool_consts, 1)
                pool.wait_ge(pool_consts, made[0])

            link(nc.gpsimd.memset(ident[:], 0.0))
            link(nc.gpsimd.affine_select(out=ident[:], in_=ident[:], compare_op=ALU.not_equal, fill=1.0, base=0,
                                         pattern=[[-1, P]], channel_multiplier=1))
            link(nc.gpsimd.memset(comb_parts[:], 1.0))
            link(nc.gpsimd.memset(sel[:], 0.0))
            for k in range(PARTS):
                link(nc.gpsimd.affine_select(out=sel[:], in_=sel[:], compare_op=ALU.not_equal, fill=1.0,
                                             base=-SHARE_PART.index(k) * NX,
                                             pattern=[[-1, NX]], channel_multiplier=1))
            for k, value in enumerate((EPS, -0.5, -1.0, 1.0 / DM)):
                link(nc.gpsimd.memset(consts[:, k:k + 1], value))
            for k in range(NX):
                link(nc.gpsimd.memset(expert_no[:, k:k + 1], float(k)))
            assert made[0] == POOL_CONSTS

            def softplus_sum(w, par):
                pool.wait_ge(softplus, 3 * w + 3)
                pool.wait_ge(sp_fix, 2 * w + 2)
                nc.gpsimd.tensor_tensor(sp_l[:], sp_l[:], sp_w, ALU.add).then_inc(sp_sum, 1)
                pool.wait_ge(sp_sum, w + 1)
                nc.gpsimd.tensor_tensor(delta[:, par, :], delta[:, par, :], sp_l[:], ALU.add).then_inc(delta_ready, 1)

            def z_affine(w):
                pool.wait_ge(z_stats, 2 * w + 2)
                wait(pool, siluz_ready, w)
                nc.gpsimd.tensor_tensor(z_ln[:, 0:1], z_mv[:, 1:2], eps, ALU.add)
                nc.gpsimd.tensor_tensor(z_ln[:, 1:2], z_mv[:, 0:1], minus_one, ALU.mult).then_inc(z_scale, 1)
                pool.wait_ge(z_scale, 3 * w + 1)
                nc.gpsimd.tensor_tensor(z_ln[:, 2:3], z_ln[:, 0:1], minus_half, ALU.pow).then_inc(z_scale, 1)
                pool.wait_ge(z_scale, 3 * w + 2)
                nc.gpsimd.tensor_tensor(z_ln[:, 3:4], z_ln[:, 1:2], z_ln[:, 2:3], ALU.mult).then_inc(z_scale, 1)

            def add_to_first(b, k):
                pool.wait_ge(paired, PAIRS * (NW * b + k // 2) + k % 2 + 2)
                nc.gpsimd.tensor_tensor(pair_sum[:, 0], pair_sum[:, 0], pair_sum[:, 1], ALU.add).then_inc(pair_added, 1)

            def residual(w, c):
                pool.wait_ge(gated, w + 1)
                pool.wait_ge(res_loaded, DMA * (w + 1))
                nc.gpsimd.tensor_tensor(x2[:, c, :], x2[:, c, :], x_res[:], ALU.add).then_inc(x2_ready, 1)

            def sum_windows(body_of, b, c):
                if c == 1 and b_ffn(body_of):
                    wait_drained(pool, body_of, "down", NE - 1)
                if c > 1:
                    pool.wait_ge(x_summed, (NW - 1) * b + c - 1)
                pool.wait_ge(x2_ready, NW * b + c + 1)
                first = x2[:, 0, :] if c == 1 else x_sum
                nc.gpsimd.tensor_tensor(x_sum, first, x2[:, c, :], ALU.add).then_inc(x_summed, 1)

            def body(b):
                for slot in range(GB):
                    c, g = slot // NG, slot % NG
                    w = NW * b + c
                    for name, k in due(b, slot, STEPS, READS):
                        if name == "add":
                            add_to_first(b, k)
                        if name == "y":
                            residual(NW * b + k - 1, (k - 1) % NW)
                            if k != 1:
                                sum_windows(b, b if k > 0 else b - 1, (k - 1) % NW)
                    if b_scan(b):
                        i = GB * b + slot
                        if g == 1:
                            z_affine(w)
                        pool.wait_ge(scanned, i + 1)
                        if c == 0:
                            pool.wait_ge(c_loaded[g], DMA * (b + 1))
                        nc.gpsimd.tensor_tensor(ring[:, slot % RING], ring[:, slot % RING], bc[:, g, 1],
                                                ALU.mult).then_inc(weighted, 1)
                    for name, k in due(b, slot + 0.5, STEPS, READS):
                        if name == "fix":
                            softplus_sum(NW * b + k + 1, (k + 1) % 2)

            each_batch(pool, body)

        @block.scalar
        def _(act):
            act.wait_ge(ssm_loaded, DMA * N_SSM)
            nc.scalar.activation(a_neg[:], a_neg[:], ACT.Exp).then_inc(act_consts, 1)
            nc.scalar.activation(gates[:, 0:1], gates[:, 0:1], ACT.Tanh).then_inc(act_consts, 1)
            act.wait_ge(pool_consts, POOL_CONSTS)
            act.wait_ge(dve_consts, 2)

            def exps(b, c, g):
                w, i = NW * b + c, GB * b + NG * c + g
                if g == 0:
                    act.wait_ge(delta_ready, w + 1)
                wait(act, scanned, i - 1)
                for n in range(PAIR):
                    last = nc.scalar.activation(decay[:, g % 2, n, 1:L], delta[:, c % 2, 1:L], ACT.Exp,
                                                scale=a_neg[:, c, PAIR * g + n:PAIR * g + n + 1])
                last.then_inc(exp_ready, 1)

            def load_ctx(m):
                act.wait_ge(u_ready, NW * m)
                apart(act)
                nc.scalar.dma_start(ctx_in[:], ctxT[m].rearrange("(k p) l -> p k l", p=P)).then_inc(ctx_loaded, DMA)

            def in_proj_out(b, c):
                bank = wait_filled(act, b, "in_proj", c)
                if not is_int(b, -1):
                    act.wait_ge(conv_step, (TAPS - 1) * (NW * (b + 1) + c))
                    act.wait_ge(sp_sum, NW * b + c + 1)
                nc.scalar.activation(padded(b, c)[:, TAPS - 1:], wk[:, bank, :], ACT.Copy)
                if not is_int(b, -1):
                    if c == NW - 1:
                        act.wait_ge(u_copied, DMA * (b + 1))
                    else:
                        act.wait_ge(skipped, NW * b + c + 1)
                nc.scalar.activation(u[:, c, :], wk[:, bank, :], ACT.Identity, scale=conv_taps[:, c, TAPS - 1:TAPS],
                                     bias=conv_bias[:, c:c + 1]).then_inc(drained[bank], 1)

            def silu_u(b, c):
                act.wait_ge(conv_step, (TAPS - 1) * (NW * (b + 1) + c + 1))
                nc.scalar.activation(u[:, c, :], u[:, c, :], ACT.Silu).then_inc(u_ready, 1)

            def silu_z(b, c):
                w = NW * b + c
                act.wait_ge(z_scale, 3 * w + 3)
                nc.scalar.activation(z[:, c % 2, :], z[:, c % 2, :], ACT.Silu, scale=z_ln[:, 2:3],
                                     bias=z_ln[:, 3:4]).then_inc(siluz_ready, 1)

            def dt_softplus(b, c):
                w, cn = NW * b + c + 1, (c + 1) % NW
                bank = wait_filled(act, b, "dt", c)
                wait(act, sp_fix, 2 * w)
                wait(act, softplus, 3 * w)
                nc.scalar.activation(sp_e[:], wk[:, bank, :], ACT.Abs, bias=dt_bias[:, cn:cn + 1]).then_inc(softplus, 1)
                wait(act, du_ready, w - 1)
                wait(act, exp_ready, NG * (w - 1))
                nc.scalar.activation(delta[:, cn % 2, :], wk[:, bank, :], ACT.Relu, bias=dt_bias[:, cn:cn + 1]).then_inc(drained[bank], 1)
                act.wait_ge(softplus, 3 * w + 1)
                nc.scalar.activation(sp_e[:], sp_e[:], ACT.Exp, scale=-1.0).then_inc(softplus, 1)
                act.wait_ge(softplus, 3 * w + 2)
                wait(act, delta_ready, w)
                nc.scalar.activation(sp_l[:], sp_e[:], ACT.Ln, bias=1.0).then_inc(softplus, 1)

            def what_is_due(b, time):
                m = b - 1
                for name, k in due(b, time, READS, STEPS):
                    if name == "in_proj":
                        in_proj_out(b, k)
                    if name == "x_proj":
                        bank = wait_filled(act, b, name)
                        wait(act, xdbl_stored, DMA * (b + 1))
                        nc.scalar.activation(x_dbl[:], wk[0:R + 2 * NS, bank, :], ACT.Copy).then_inc(drained[bank], 1)
                    if name == "dt":
                        dt_softplus(b, k)
                    if name == "var":
                        bank = wait_filled(act, b, name)
                        nc.scalar.activation(rstd[:], wk[:, bank, :], ACT.Ln, bias=eps).then_inc(drained[bank], 1)
                        wait_drained(act, b, name)
                        nc.scalar.activation(rstd[:], rstd[:], ACT.Exp, scale=-0.5).then_inc(rstd_ready, 1)
                    if name == "comb":
                        bank = wait_filled(act, b, name)
                        nc.scalar.activation(comb_parts[0:NC, :], wk[0:NC, bank, :], ACT.Copy).then_inc(drained[bank], 1)
                    if name == "share_exp":
                        act.wait_ge(route_step, ROUTE_STEPS * m + 4)
                        nc.scalar.activation(share[:, 1], share[:, 0], ACT.Exp).then_inc(route_exp, 1)
                    if name == "square":
                        wait_drained(act, b, "mean")
                        wait(act, out_stored[(NW - 1) % 2], DMA * (2 * m + 1))
                        nc.scalar.activation(squares, xc[:], ACT.Square).then_inc(squared, 1)
                    if name == "silu_z":
                        silu_z(b, k)
                    if name == "silu_u":
                        silu_u(b, k)
                        if is_int(b, -1) and k == NW - 1:
                            load_ctx(1)
                    if name == "gelu":
                        first, end = GELUS[k]
                        for j in range(max(first, end - 3), end):
                            wait_drained(act, b, "down", j)
                        for j in range(first, end):
                            last = nc.scalar.activation(h[:, j, :], h[:, j, :], ACT.Gelu, bias=b_down[:, j:j + 1])
                        last.then_inc(gelu_done, 1)

            def body(b):
                if b_prep(b) and not is_int(b, -1) and not is_int(b, 0):
                    load_ctx(b + 1)
                for slot in range(GB):
                    what_is_due(b, slot)
                    if b_scan(b):
                        if slot < GB - 1:
                            exps(b, (slot + 1) // NG, (slot + 1) % NG)
                        elif not is_int(b, NB - 1):
                            exps(b + 1, 0, 0)
                    what_is_due(b, slot + 0.5)
                if is_int(b, -1):
                    exps(0, 0, 0)
                if is_int(b, 0):
                    act.wait_ge(ffn_loaded, DMA * N_FFN)
                    nc.scalar.activation(gates[:, 1:2], gates[:, 1:2], ACT.Tanh).then_inc(act_consts, 1)

            each_batch(act, body)

        @block.vector
        def _(dve):
            nc.vector.memset(xpad[:, 0:TAPS - 1], 0.0)
            for c in range(NW):
                nc.vector.memset(padded(-1, c)[:, 0:TAPS - 1], 0.0)
            nc.vector.memset(decay[:, :, :, 0:1], 0.0).then_inc(dve_consts, 1)
            dve.wait_ge(act_consts, 1)
            nc.vector.tensor_scalar(a_neg[:], a_neg[:], -1.0, None, ALU.mult).then_inc(dve_consts, 1)

            def delta_u(b, c):
                w = NW * b + c
                dve.wait_ge(delta_ready, w + 1)
                u_there(dve, b, c)
                wait(dve, outer_ready, NG * w)
                nc.vector.tensor_tensor(du[:], delta[:, c % 2, :], u[:, u_place(c), :], ALU.mult).then_inc(du_ready, 1)
                dve.wait_ge(du_ready, w + 1)

            def outer(b, c, g):
                if g == 0:
                    delta_u(b, c)
                slot = (NG * c + g) % RING
                if c == 0:
                    dve.wait_ge(b_loaded[g], DMA * (b + 1))
                wait(dve, paired, (GB // 2) * b + (NG * c + g - RING) // 2 + 1)
                nc.vector.tensor_tensor(ring[:, slot], du[:, None, :].broadcast_to([P, PAIR, L]), bc[:, g, 0],
                                        ALU.mult).then_inc(outer_ready, 1)

            def scan(b, c, g):
                i = GB * b + NG * c + g
                slot = (NG * c + g) % RING
                dve.wait_ge(outer_ready, i + 1)
                dve.wait_ge(exp_ready, i + 1)
                states = ring[:, slot].rearrange("p n l -> p (n l)")
                nc.vector.tensor_tensor_scan(states, decay[:, g % 2].rearrange("p n l -> p (n l)"), states, 0.0,
                                             ALU.mult, ALU.add).then_inc(scanned, 1)

            def skip(b, c):
                w, slot = NW * b + c, NG * c % RING
                dve.wait_ge(weighted, NG * w + 1)
                nc.vector.scalar_tensor_tensor(ring[:, slot, 0, :], u[:, u_place(c), :], d_skip[:, c:c + 1],
                                               ring[:, slot, 0, :], ALU.mult, ALU.add).then_inc(skipped, 1)

            def add_pair(b, k):
                slot, c, r = k % RING, k // NG, k // 2 % PAIRS
                if r == 0:
                    if windows_before(b, c):
                        wait_filled(dve, b, "y", c)
                elif r > 1:
                    dve.wait_ge(pair_added, 2 * (NW * b + c) + r - 1)
                dve.wait_ge(weighted, GB * b + k + 2)
                if k % NG == 0:
                    dve.wait_ge(skipped, NW * b + k // NG + 1)
                nc.vector.tensor_tensor(pair_sum[:, min(r, 1)], ring[:, slot], ring[:, slot + 1], ALU.add).then_inc(paired, 1)

            def conv(b, c):
                wait_drained(dve, b, "in_proj", c)
                for k in range(TAPS - 1):
                    nc.vector.scalar_tensor_tensor(u[:, c, :], padded(b, c)[:, k:k + L], conv_taps[:, c, k:k + 1], u[:, c, :],
                                                   ALU.mult, ALU.add).then_inc(conv_step, 1)
                    if k < TAPS - 2:
                        dve.wait_ge(conv_step, (TAPS - 1) * (NW * (b + 1) + c) + k + 1)

            def stats_z(b, c):
                w = NW * b + c
                dve.wait_ge(z_loaded[c % 2], DMA * (2 * b + c // 2 + 1))
                wait(dve, z_scale, 3 * w)
                nc.vector.bn_stats(z_stat[:], z[:, c % 2, :]).then_inc(z_stats, 1)
                dve.wait_ge(z_stats, 2 * w + 1)
                apart(dve)
                nc.vector.bn_aggr(z_mv, z_stat[:]).then_inc(z_stats, 1)

            def gate(b, k):
                w, c = NW * b + k - 1, (k - 1) % NW
                bank = wait_filled(dve, b, "y", k)
                dve.wait_ge(siluz_ready, w + 1)
                if not is_int(b, 0) and k > 0:
                    dve.wait_ge(x2_stored, DMA * b)
                nc.vector.scalar_tensor_tensor(x2[:, c, :], wk[:, bank, :], gates[:, 0:1], z[:, c % 2, :], ALU.mult,
                                               ALU.mult).then_inc(drained[bank], 1)
                wait_drained(dve, b, "y", k)
                dve.sem_inc(gated, 1)

            def softplus_fix(b, c):
                w = NW * b + c + 1
                dve.wait_ge(softplus, 3 * w + 2)
                if b_prep(b):
                    dve.wait_ge(conv_step, (TAPS - 1) * (NW * (b + 1) + c + 1))
                nc.vector.tensor_scalar(sp_w, sp_e[:], 1.0, -1.0, ALU.add, ALU.add).then_inc(sp_fix, 1)
                dve.wait_ge(sp_fix, 2 * w + 1)
                nc.vector.scalar_tensor_tensor(sp_w, sp_w, -1.0, sp_e[:], ALU.mult, ALU.add).then_inc(sp_fix, 1)

            def split_biases():
                def link(ins):
                    link.made += 1
                    ins.then_inc(bias_step, 1)
                    dve.wait_ge(bias_step, link.made)

                link.made = 0
                dve.wait_ge(bias_loaded, DMA * N_BIAS)
                link(nc.vector.tensor_copy(b_up[:], bias_rows))
                link(nc.vector.tensor_tensor(bias_rest, bias_rows, b_up[:], ALU.subtract))
                link(nc.vector.tensor_scalar(bias_sum, b_up[:], part_mask[:, 0:1], None, ALU.mult))
                link(nc.vector.tensor_copy(b_up[:], bias_rest))
                link(nc.vector.tensor_tensor(bias_rows, bias_rest, b_up[:], ALU.subtract))
                link(nc.vector.scalar_tensor_tensor(bias_sum, b_up[:], part_mask[:, 1:2], bias_sum, ALU.mult, ALU.add))
                link(nc.vector.scalar_tensor_tensor(b_up[:], bias_rows, part_mask[:, 2:3], bias_sum, ALU.mult, ALU.add))
                assert link.made == BIAS_STEPS

            def centre(b):
                bank = wait_filled(dve, b, "mean")
                nc.vector.tensor_tensor(xc[:], x2[:], wk[:, bank, None, :].broadcast_to([P, NW, L]),
                                        ALU.subtract).then_inc(drained[bank], 1)
                wait_drained(dve, b, "mean")

            def down_out(b, k):
                bank = wait_filled(dve, b, "down", k)
                if k == 0:
                    dve.wait_ge(rstd_ready, b)
                nc.vector.tensor_tensor(h[:, k, :], wk[:, bank, :], rstd[:], ALU.mult).then_inc(drained[bank], 1)

            def over_experts(t):
                return t.broadcast_to([P, NT, NX])

            def stepper(b, done):
                steps = [done]

                def step(ins):
                    steps[0] += 1
                    ins.then_inc(route_step, 1)

                def settle():
                    dve.wait_ge(route_step, ROUTE_STEPS * (b - 1) + steps[0])
                return step, settle, steps

            def scale_out(b):
                bank = wait_filled(dve, b, "scale")
                nc.vector.tensor_copy(rstd_col[:].rearrange("p t o -> p (t o)"), wk[:, bank, 0:NT]).then_inc(drained[bank], 1)

            def pick_experts(b):
                step, settle, steps = stepper(b, 0)
                bank = wait_filled(dve, b, "logits")
                wait_drained(dve, b, "scale")
                nc.vector.tensor_tensor(logit[:], wk[:, bank, 0:NT * NX].rearrange("p (t x) -> p t x", t=NT),
                                        rstd_col[:].broadcast_to([P, NT, NX]), ALU.mult).then_inc(drained[bank], 1)
                wait_drained(dve, b, "logits")
                apart(dve)
                for t in range(NT):
                    last = nc.vector.max(top[:, t, :], logit[:, t, :])
                step(last)
                settle()
                apart(dve)
                for t in range(NT):
                    last = nc.vector.max_index(top_no[:, t, :], top[:, t, :], logit[:, t, :])
                step(last)
                settle()
                step(nc.vector.tensor_copy(top_f[:], top_no[:, :, 0:2]))
                step(nc.vector.tensor_tensor(share[:, 0], top[:, :, 1:2], top[:, :, 0:1], ALU.subtract))
                settle()
                numbers = expert_no[:, None, :].broadcast_to([P, NT, NX])
                step(nc.vector.tensor_tensor(pick[:, 0], numbers, over_experts(top_f[:, :, 0:1]), ALU.is_equal))
                step(nc.vector.tensor_tensor(pick[:, 1], numbers, over_experts(top_f[:, :, 1:2]), ALU.is_equal))
                assert steps[0] == PICK_STEPS

            def shares(b):
                step, settle, steps = stepper(b, PICK_STEPS)
                dve.wait_ge(route_exp, b)
                settle()
                step(nc.vector.tensor_scalar(share[:, 2], share[:, 1], 1.0, None, ALU.add))
                step(nc.vector.tensor_tensor(pick[:, 1], pick[:, 1], over_experts(share[:, 1]), ALU.mult))
                settle()
                step(nc.vector.reciprocal(share[:, 2], share[:, 2]))
                step(nc.vector.tensor_tensor(pick[:, 2], pick[:, 0], pick[:, 1], ALU.add))
                settle()
                step(nc.vector.tensor_tensor(pick[:, 2], pick[:, 2], over_experts(share[:, 2]), ALU.mult))
                settle()
                step(nc.vector.tensor_copy(part16[:, 0], pick[:, 2]))
                settle()
                step(nc.vector.tensor_tensor(pick[:, 0], pick[:, 2], part16[:, 0], ALU.subtract))
                step(nc.vector.tensor_copy(parts[:, :, 0:3, :], part16[:, 0, :, None, :].broadcast_to([P, NT, 3, NX])))
                settle()
                step(nc.vector.tensor_copy(part16[:, 1], pick[:, 0]))
                settle()
                step(nc.vector.tensor_tensor(parts[:, :, 5, :], pick[:, 0], part16[:, 1], ALU.subtract))
                step(nc.vector.tensor_copy(parts[:, :, 3:5, :], part16[:, 1, :, None, :].broadcast_to([P, NT, 2, NX])))
                assert steps[0] == ROUTE_STEPS, steps

            def mix(b, k):
                m = b - 1
                bank = wait_filled(dve, b, "mix", k)
                dve.wait_ge(gelu_done, len(GELUS) * m + [k < end for _, end in GELUS].index(True) + 1)
                nc.vector.tensor_tensor(h[:, k, :], h[:, k, :], wk[:, bank, :], ALU.mult).then_inc(drained[bank], 1)

            def up_out(b, d):
                m = b - 1
                bank = wait_filled(dve, b, "up", d)
                dve.wait_ge(x2_loaded[d % 2], DMA * (2 * m + d // 2 + 1))
                nc.vector.scalar_tensor_tensor(x_out[:, d % 2, :], wk[:, bank, :], gates[:, 1:2], x_out[:, d % 2, :],
                                               ALU.mult, ALU.add).then_inc(drained[bank], 1)

            def what_is_due(b, time):
                for name, k in due(b, time, READS, STEPS):
                    if name == "y":
                        gate(b, k)
                    if name == "skip":
                        skip(b, k)
                    if name == "conv":
                        conv(b, k)
                    if name == "fix":
                        softplus_fix(b, k)
                    if name == "mean":
                        centre(b)
                    if name == "down":
                        down_out(b, k)
                    if name == "scale":
                        scale_out(b)
                    if name == "logits":
                        pick_experts(b)
                    if name == "shares":
                        shares(b)
                    if name == "mix":
                        mix(b, k)
                    if name == "up":
                        up_out(b, k)

            def body(b):
                for slot in range(GB):
                    c, g = slot // NG, slot % NG
                    what_is_due(b, slot)
                    if b_scan(b):
                        if slot < GB - 1:
                            outer(b, (slot + 1) // NG, (slot + 1) % NG)
                        elif not is_int(b, NB - 1):
                            outer(b + 1, 0, 0)
                        scan(b, c, g)
                        if g == 0:
                            stats_z(b, c)
                    if slot % 2 == 0:
                        k = slot - LAG
                        if k >= 0 and b_scan(b):
                            add_pair(b, k)
                        elif k < 0 and b_ffn(b):
                            add_pair(b - 1, GB + k)
                    what_is_due(b, slot + 0.5)
                    if is_int(b, -1) and slot == NG:
                        split_biases()
                if is_int(b, -1):
                    outer(0, 0, 0)
                if is_int(b, 0):
                    dve.wait_ge(act_consts, 3)

            dve.wait_ge(act_consts, 2)
            each_batch(dve, body)

        @block.tensor
        def _(pe):
            pe.wait_ge(in_w_loaded, DMA)

            def job(b, name, k):
                m = b - 1
                bank, n = work(b, name, k)
                wait(pe, drained[bank], n - 1)
                o = wk[:, bank, :]
                if name == "y":
                    pe.wait_ge(pair_added, 2 * (NW * b + k))
                    for j in range(PAIR):
                        nc.tensor.matmul(o, ident[:], pair_sum[:, 0, j, :], start=j == 0, stop=False)
                    pe.wait_ge(paired, PAIRS * (NW * b + k))
                    for j in range(PAIR):
                        last = nc.tensor.matmul(o, ident[:], pair_sum[:, 1, j, :], start=False, stop=j == PAIR - 1)
                if name == "in_proj":
                    if k == 0:
                        pe.wait_ge(ctx_loaded, DMA * (b + 2))
                    for j in range(KC):
                        last = nc.tensor.matmul(o, in_w[:, j, k * P:(k + 1) * P], ctx_in[:, j, :], start=j == 0, stop=j == KC - 1)
                if name == "x_proj":
                    if is_int(b, -1):
                        pe.wait_ge(ssm_loaded, DMA * N_SSM)
                        pe.wait_ge(pool_consts, POOL_CONSTS)
                    for j in range(NW):
                        pe.wait_ge(u_ready, NW * (b + 1) + j + 1)
                        last = nc.tensor.matmul(o[0:R + 2 * NS, :], xp_w[:, j, :], u[:, j, :], start=j == 0, stop=j == NW - 1)
                if name == "dt":
                    if k == NW - 1:
                        wait_drained(pe, b, "x_proj")
                    kn = (k + 1) % NW
                    last = nc.tensor.matmul(o, dt_w[:, kn * P:(kn + 1) * P], x_dbl[0:R, :], start=True, stop=True)
                if name == "mean":
                    pe.wait_ge(x_summed, (NW - 1) * b)
                    last = nc.tensor.matmul(o, mean_w, x_sum, start=True, stop=True)
                if name == "var":
                    pe.wait_ge(squared, m + 1)
                    for j in range(NW):
                        last = nc.tensor.matmul(o, mean_w, squares[:, j, :], start=j == 0, stop=j == NW - 1)
                if name == "scale":
                    pe.wait_ge(rstd_ready, m + 1)
                    for t in range(NT):
                        last = nc.tensor.matmul(o[:, t:t + 1], rstd[:, t * P:(t + 1) * P], ident[:, 0:1], start=True, stop=True)
                if name == "logits":
                    for t in range(NT):
                        for j in range(NW):
                            last = nc.tensor.matmul(o[:, t * NX:(t + 1) * NX], xc[:, j, t * P:(t + 1) * P], gate_w[:, j, :],
                                                    start=j == 0, stop=j == NW - 1)
                if name == "comb":
                    pe.wait_ge(route_step, ROUTE_STEPS * b)
                    apart(pe)
                    for t in range(NT):
                        last = nc.tensor.transpose(o[0:NC, t * P:(t + 1) * P],
                                                   parts[:, t].rearrange("p i x -> p (i x)"), ident[:])
                if name == "down":
                    if k == 0:
                        wait_drained(pe, b, "mean")
                    for j in range(NW):
                        last = nc.tensor.matmul(o, w_down[:, j, k, :], xc[:, j, :], start=j == 0, stop=j == NW - 1)
                if name == "mix":
                    if k == 0:
                        wait_drained(pe, b, "comb")
                    last = nc.tensor.matmul(o, sel[:, k:k + 1].broadcast_to([NR, P]), comb_parts[:], start=True, stop=True)
                if name == "up":
                    if k == 0:
                        wait_mixed(b, bank, UP_SPLIT, NX)
                        pe.wait_ge(gelu_done, len(GELUS) * b)
                    for j in range(UP_SPLIT, NE):
                        last = nc.tensor.matmul(o, w_up[:, j, k * P:(k + 1) * P], h[:, j, :], start=False, stop=j == NE - 1)
                last.then_inc(filled[bank], 1)

            def wait_mixed(b, bank, first, end):
                last = [k for k in range(first, end) if work(b, "mix", k)[0] != bank]
                if last:
                    wait_drained(pe, b, "mix", last[-1])

            def start_up(b, k):
                bank, n = work(b, "up", k)
                wait(pe, drained[bank], n - 1)
                if k == 0:
                    wait_mixed(b, bank, 0, UP_SPLIT)
                nc.tensor.matmul(wk[:, bank, :], b_up[:, k * P:(k + 1) * P], comb_parts[:], start=True, stop=False)
                for j in range(UP_SPLIT):
                    nc.tensor.matmul(wk[:, bank, :], w_up[:, j, k * P:(k + 1) * P], h[:, j, :], start=False, stop=False)

            def body(b):
                for slot in range(GB):
                    for name, k in due(b, slot, JOBS, STEPS):
                        if name == "start_up":
                            start_up(b, k)
                        elif name in JOBS:
                            job(b, name, k)
                if is_int(b, 0):
                    pe.wait_ge(ffn_loaded, DMA * N_FFN)
                    pe.wait_ge(bias_step, BIAS_STEPS)

            each_batch(pe, body)


_INS = ['x', 'xT', 'ctxT', 'g_xattn', 'g_ffn', 'in_wT', 'conv_w', 'conv_b', 'xp_wT', 'dt_wT', 'dt_b', 'A_log', 'D',
        'gate_wT', 'wdT', 'bdT', 'wuT', 'bu', 'ws_dT', 'bs_d', 'ws_uT', 'bs_u', 'mask']


def kernel(x, ctx_1024, g_xattn, g_ffn, L0_xattn_in_proj_w, L0_xattn_conv_w, L0_xattn_conv_b, L0_xattn_x_proj_w,
           L0_xattn_dt_proj_w, L0_xattn_dt_proj_b, L0_xattn_A_log, L0_xattn_D, L0_ffn_gate_w, L0_ffn_wd, L0_ffn_bd,
           L0_ffn_wu, L0_ffn_bu, L0_ffn_ws_d, L0_ffn_bs_d, L0_ffn_ws_u, L0_ffn_bs_u):
    import numpy as np
    import concourse.bacc as bacc
    from concourse.bass_utils import run_bass_kernel_spmd

    def by_partition(t):
        t = np.asarray(t)
        return np.swapaxes(t.reshape((NW, P) + t.shape[1:]), 0, 1)

    laid = {
        'x': x, 'xT': np.transpose(x, (0, 2, 1)), 'ctxT': np.transpose(ctx_1024, (0, 2, 1)),
        'g_xattn': g_xattn, 'g_ffn': g_ffn, 'in_wT': np.transpose(L0_xattn_in_proj_w),
        'conv_w': by_partition(L0_xattn_conv_w), 'conv_b': by_partition(L0_xattn_conv_b), 'xp_wT': np.transpose(L0_xattn_x_proj_w),
        'dt_wT': np.transpose(L0_xattn_dt_proj_w), 'dt_b': by_partition(L0_xattn_dt_proj_b), 'A_log': by_partition(L0_xattn_A_log),
        'D': by_partition(L0_xattn_D), 'gate_wT': np.transpose(L0_ffn_gate_w), 'wdT': np.transpose(L0_ffn_wd, (2, 0, 1)),
        'bdT': np.transpose(L0_ffn_bd), 'wuT': np.transpose(L0_ffn_wu, (2, 0, 1)), 'bu': L0_ffn_bu,
        'ws_dT': np.transpose(L0_ffn_ws_d), 'bs_d': L0_ffn_bs_d, 'ws_uT': np.transpose(L0_ffn_ws_u),
        'bs_u': L0_ffn_bs_u,
        'mask': np.eye(PARTS, dtype=np.float32)[[part for part in BIAS_PART for _ in range(NX)] + list(range(PARTS))],
    }
    nc = bacc.Bacc("TRN2", target_bir_lowering=False, num_devices=1)
    arrays, args = {}, []
    for name in _INS:
        a = np.ascontiguousarray(laid[name])
        arrays[f"in_{name}"] = a
        args.append(nc.dram_tensor(f"in_{name}", a.shape, mybir.dt.from_np(a.dtype), kind="ExternalInput").ap())
    out = nc.dram_tensor("out_T", (NB, DM, L), F32, kind="ExternalOutput").ap()
    mamba_moe_kernel(nc, *args, out)
    r = run_bass_kernel_spmd(nc, [arrays], core_ids=[0])
    return np.ascontiguousarray(np.transpose(r.results[0]["out_T"], (0, 2, 1)))
```
